# Optimizing a Trainium2 kernel written in Bass

```python
import numpy as np
import jax
import jax.numpy as jnp

def _softmax(x, axis=-1):
    return jax.nn.softmax(x, axis=axis)

def _gelu(x):
    return jax.nn.gelu(x, approximate=True)

def _silu(x):
    return jax.nn.silu(x)

def _sigmoid(x):
    return jax.nn.sigmoid(x)

def _layernorm(x, axis=-1, eps=1e-05):
    m = jnp.mean(x, axis=axis, keepdims=True)
    v = jnp.var(x, axis=axis, keepdims=True)
    return (x - m) / jnp.sqrt(v + eps)

def _scatter_add(tgt, idx, src, axis=0):
    return tgt.at[idx].add(src)

def _segment_sum(src, seg, n):
    return jax.ops.segment_sum(src, seg, n)
kernel_name = 'mk_macaron_d2_jaxref_r8_249a4c'

def setup_inputs(seed: int=0):
    np.random.seed(seed)
    _w = jnp.asarray

    def _L0_attn_setup():
        import jax, jax.numpy as jnp
        import numpy as np
        DIM = 128
        B, N = (8, 512)
        EPS = 1e-06
        key = jax.random.key(seed)
        k1, k2, k3, k4 = jax.random.split(key, 4)
        x = jax.random.normal(k1, (B, N, DIM), dtype=jnp.float32)
        s = 1.0 / np.sqrt(DIM)
        W_qkv = jax.random.uniform(k2, (3 * DIM, DIM), jnp.float32, -s, s)
        W_out = jax.random.uniform(k3, (DIM, DIM), jnp.float32, -s, s)
        b_out = jax.random.uniform(k4, (DIM,), jnp.float32, -s, s)
        return {'x': x, 'W_qkv': W_qkv, 'W_out': W_out, 'b_out': b_out}
    _L0_attn_in = _L0_attn_setup()

    def _L0_ffn_setup():
        import jax, jax.numpy as jnp
        import numpy as np
        DIM = 128
        DEPTH = 6
        HEADS = 16
        DIM_HEAD = 64
        WINDOW = 32
        INNER = HEADS * DIM_HEAD
        DIM_INNER = int(DIM * 4 * 2 / 3)
        QK_SCALE = 8.0

        def shift_tokens(t):
            a, s = jnp.split(t, 2, -1)
            s = jnp.pad(s, ((0, 0), (1, 0), (0, 0)))[:, :-1]
            return jnp.concatenate([a, s], -1)

        def l2norm(t):
            return t / jnp.maximum(jnp.linalg.norm(t, axis=-1, keepdims=True), 1e-12)

        def rotate_half(x):
            x1, x2 = jnp.split(x, 2, -1)
            return jnp.concatenate([-x2, x1], -1)

        def rotary_tables(n):
            half = jnp.arange(0, DIM_HEAD, 2, dtype=jnp.float32)
            inv_freq = 1.0 / 10000.0 ** (half / DIM_HEAD)
            t = jnp.arange(n, dtype=jnp.float32)
            freqs = t[:, None] * inv_freq[None, :]
            freqs = jnp.concatenate([freqs, freqs], -1)
            base_scale = (half + 0.4 * DIM_HEAD) / (1.4 * DIM_HEAD)
            power = (t - n // 2) / (WINDOW // 2)
            scale = base_scale[None, :] ** power[:, None]
            scale = jnp.concatenate([scale, scale], -1)
            return (freqs, scale)

        def local_attention(q, k, v):
            b, h, n, d = q.shape
            w = WINDOW
            nw = n // w
            bq = q.reshape(b, h, nw, w, d)
            bk = k.reshape(b, h, nw, w, d)
            bv = v.reshape(b, h, nw, w, d)

            def look(t):
                p = jnp.pad(t, ((0, 0), (0, 0), (1, 0), (0, 0), (0, 0)))
                return jnp.concatenate([p[:, :, :nw], p[:, :, 1:]], axis=3)
            bk2, bv2 = (look(bk), look(bv))
            seq = jnp.arange(n).reshape(nw, w)
            seq_p = jnp.pad(seq, ((1, 0), (0, 0)), constant_values=-1)
            jt = jnp.concatenate([seq_p[:nw], seq_p[1:]], axis=1)
            it = seq[:, :, None]
            jb = jt[:, None, :]
            mask = (it < jb) | (it > jb + w) | (jb == -1)
            sim = jnp.einsum('bhwie,bhwje->bhwij', bq, bk2) * QK_SCALE
            sim = jnp.where(mask, -jnp.finfo(sim.dtype).max, sim)
            attn = jax.nn.softmax(sim, -1)
            out = jnp.einsum('bhwij,bhwje->bhwie', attn, bv2)
            return out.reshape(b, h, n, d)

        def attn_layer(x, Wqkv, qs, ksc, Wo):
            b, n, _ = x.shape
            qkv = x @ Wqkv
            q, k, v = jnp.split(qkv, 3, -1)
            sh = lambda t: t.reshape(b, n, HEADS, DIM_HEAD).transpose(0, 2, 1, 3)
            q, k, v = (sh(q), sh(k), sh(v))
            q = l2norm(q) * qs
            k = l2norm(k) * ksc
            freqs, scale = rotary_tables(n)
            cos, sin = (jnp.cos(freqs), jnp.sin(freqs))
            q = q * cos * scale + rotate_half(q) * sin * scale
            inv = 1.0 / scale
            k = k * cos * inv + rotate_half(k) * sin * inv
            out = local_attention(q, k, v)
            out = out.transpose(0, 2, 1, 3).reshape(b, n, INNER)
            return out @ Wo

        def ffn_layer(x, g, bln, W1, b1, W2, b2):
            mu = x.mean(-1, keepdims=True)
            var = ((x - mu) ** 2).mean(-1, keepdims=True)
            xn = (x - mu) / jnp.sqrt(var + 1e-05) * g + bln
            hg = xn @ W1 + b1
            a, gate = jnp.split(hg, 2, -1)
            return a * jax.nn.gelu(gate, approximate=False) @ W2 + b2
        key = jax.random.key(seed)
        ks = jax.random.split(key, 8)
        B, N = (2, 256)
        init = lambda k, shape: jax.random.normal(k, shape, jnp.float32) * 0.02
        return {'x': jax.random.normal(ks[0], (B, N, DIM), jnp.float32), 'Wqkv': init(ks[1], (DEPTH, DIM, 3 * INNER)), 'q_scale': jnp.ones((DEPTH, DIM_HEAD), jnp.float32), 'k_scale': jnp.ones((DEPTH, DIM_HEAD), jnp.float32), 'Wo': init(ks[2], (DEPTH, INNER, DIM)), 'ln_g': jnp.ones((DEPTH, DIM), jnp.float32), 'ln_b': jnp.zeros((DEPTH, DIM), jnp.float32), 'W1': init(ks[3], (DEPTH, DIM, 2 * DIM_INNER)), 'b1': jnp.zeros((DEPTH, 2 * DIM_INNER), jnp.float32), 'W2': init(ks[4], (DEPTH, DIM_INNER, DIM)), 'b2': jnp.zeros((DEPTH, DIM), jnp.float32)}
    _L0_ffn_in = _L0_ffn_setup()

    def _L1_attn_setup():
        import jax, jax.numpy as jnp
        import numpy as np
        D_MODEL = 128
        NUM_HEADS = 16
        D_K = D_MODEL // NUM_HEADS

        def _layer_norm(y, g, b, eps=1e-05):
            mu = jnp.mean(y, axis=-1, keepdims=True)
            var = jnp.var(y, axis=-1, keepdims=True)
            return (y - mu) * jax.lax.rsqrt(var + eps) * g + b
        key = jax.random.key(seed)
        ks = jax.random.split(key, 7)
        B, S = (4, 256)
        lim = float(np.sqrt(6.0 / (D_MODEL + D_MODEL)))
        x = jax.random.normal(ks[0], (B, S, D_MODEL), dtype=jnp.float32)
        w_q = jax.random.uniform(ks[1], (D_MODEL, D_MODEL), jnp.float32, -lim, lim)
        w_k = jax.random.uniform(ks[2], (D_MODEL, D_MODEL), jnp.float32, -lim, lim)
        w_v = jax.random.uniform(ks[3], (D_MODEL, D_MODEL), jnp.float32, -lim, lim)
        w_o = jax.random.uniform(ks[4], (D_MODEL, D_MODEL), jnp.float32, -lim, lim)
        b_o = jnp.zeros((D_MODEL,), jnp.float32)
        ln_g = jnp.ones((D_MODEL,), jnp.float32)
        ln_b = jnp.zeros((D_MODEL,), jnp.float32)
        return {'x': x, 'w_q': w_q, 'w_k': w_k, 'w_v': w_v, 'w_o': w_o, 'b_o': b_o, 'ln_g': ln_g, 'ln_b': ln_b}
    _L1_attn_in = _L1_attn_setup()

    def _L1_ffn_setup():
        import jax, jax.numpy as jnp
        import numpy as np
        DIM = 128
        MLP_MULT = 4
        NUM_EXPERTS = 8
        EXPERT_HIDDEN = MLP_MULT * DIM // NUM_EXPERTS
        key = jax.random.key(seed)
        k_x, k_r, k_fc, k_pj = jax.random.split(key, 4)
        x = jax.random.normal(k_x, (4, 512, DIM), dtype=jnp.float32)
        w_router = jax.random.normal(k_r, (NUM_EXPERTS, DIM), dtype=jnp.float32) * (1.0 / np.sqrt(DIM))
        w_fc = jax.random.normal(k_fc, (NUM_EXPERTS, EXPERT_HIDDEN, DIM), dtype=jnp.float32) * (1.0 / np.sqrt(DIM))
        w_proj = jax.random.normal(k_pj, (NUM_EXPERTS, DIM, EXPERT_HIDDEN), dtype=jnp.float32) * (1.0 / np.sqrt(EXPERT_HIDDEN))
        return {'x': x, 'w_router': w_router, 'w_fc': w_fc, 'w_proj': w_proj}
    _L1_ffn_in = _L1_ffn_setup()
    _d = {'L0_attn_x': _L0_attn_in['x'], 'L0_attn_W_qkv': _L0_attn_in['W_qkv'], 'L0_attn_W_out': _L0_attn_in['W_out'], 'L0_attn_b_out': _L0_attn_in['b_out'], 'L0_ffn_Wqkv': _L0_ffn_in['Wqkv'], 'L0_ffn_q_scale': _L0_ffn_in['q_scale'], 'L0_ffn_k_scale': _L0_ffn_in['k_scale'], 'L0_ffn_Wo': _L0_ffn_in['Wo'], 'L0_ffn_ln_g': _L0_ffn_in['ln_g'], 'L0_ffn_ln_b': _L0_ffn_in['ln_b'], 'L0_ffn_W1': _L0_ffn_in['W1'], 'L0_ffn_b1': _L0_ffn_in['b1'], 'L0_ffn_W2': _L0_ffn_in['W2'], 'L0_ffn_b2': _L0_ffn_in['b2'], 'L1_attn_w_q': _L1_attn_in['w_q'], 'L1_attn_w_k': _L1_attn_in['w_k'], 'L1_attn_w_v': _L1_attn_in['w_v'], 'L1_attn_w_o': _L1_attn_in['w_o'], 'L1_attn_b_o': _L1_attn_in['b_o'], 'L1_attn_ln_g': _L1_attn_in['ln_g'], 'L1_attn_ln_b': _L1_attn_in['ln_b'], 'L1_ffn_w_router': _L1_ffn_in['w_router'], 'L1_ffn_w_fc': _L1_ffn_in['w_fc'], 'L1_ffn_w_proj': _L1_ffn_in['w_proj']}
    _x0 = _d['L0_attn_x']
    _d['L0_attn_x'] = jax.random.normal(jax.random.fold_in(jax.random.key(seed), 1), (2, 1024, 128), dtype=_x0.dtype)
    del _x0
    return _d

def reference(L0_attn_x, L0_attn_W_qkv, L0_attn_W_out, L0_attn_b_out, L0_ffn_Wqkv, L0_ffn_q_scale, L0_ffn_k_scale, L0_ffn_Wo, L0_ffn_ln_g, L0_ffn_ln_b, L0_ffn_W1, L0_ffn_b1, L0_ffn_W2, L0_ffn_b2, L1_attn_w_q, L1_attn_w_k, L1_attn_w_v, L1_attn_w_o, L1_attn_b_o, L1_attn_ln_g, L1_attn_ln_b, L1_ffn_w_router, L1_ffn_w_fc, L1_ffn_w_proj):

    def _L0_attn_ref(x, W_qkv, W_out, b_out):
        import jax, jax.numpy as jnp
        import numpy as np
        DIM = 128
        B, N = (8, 512)
        EPS = 1e-06
        qkv = jnp.einsum('bnd,ed->bne', x, W_qkv)
        q, k, v = jnp.split(qkv, 3, axis=-1)
        q = jax.nn.relu(q) + EPS
        k = jax.nn.relu(k) + EPS
        kv = jnp.einsum('bnd,bne->bde', k, v)
        z = 1.0 / (jnp.einsum('bnd,bd->bn', q, k.sum(axis=1)) + EPS)
        attn = jnp.einsum('bnd,bde,bn->bne', q, kv, z)
        return jnp.einsum('bne,fe->bnf', attn, W_out) + b_out

    def _L0_ffn_ref(x, Wqkv, q_scale, k_scale, Wo, ln_g, ln_b, W1, b1, W2, b2):
        import jax, jax.numpy as jnp
        import numpy as np
        DIM = 128
        DEPTH = 6
        HEADS = 16
        DIM_HEAD = 64
        WINDOW = 32
        INNER = HEADS * DIM_HEAD
        DIM_INNER = int(DIM * 4 * 2 / 3)
        QK_SCALE = 8.0

        def shift_tokens(t):
            a, s = jnp.split(t, 2, -1)
            s = jnp.pad(s, ((0, 0), (1, 0), (0, 0)))[:, :-1]
            return jnp.concatenate([a, s], -1)

        def l2norm(t):
            return t / jnp.maximum(jnp.linalg.norm(t, axis=-1, keepdims=True), 1e-12)

        def rotate_half(x):
            x1, x2 = jnp.split(x, 2, -1)
            return jnp.concatenate([-x2, x1], -1)

        def rotary_tables(n):
            half = jnp.arange(0, DIM_HEAD, 2, dtype=jnp.float32)
            inv_freq = 1.0 / 10000.0 ** (half / DIM_HEAD)
            t = jnp.arange(n, dtype=jnp.float32)
            freqs = t[:, None] * inv_freq[None, :]
            freqs = jnp.concatenate([freqs, freqs], -1)
            base_scale = (half + 0.4 * DIM_HEAD) / (1.4 * DIM_HEAD)
            power = (t - n // 2) / (WINDOW // 2)
            scale = base_scale[None, :] ** power[:, None]
            scale = jnp.concatenate([scale, scale], -1)
            return (freqs, scale)

        def local_attention(q, k, v):
            b, h, n, d = q.shape
            w = WINDOW
            nw = n // w
            bq = q.reshape(b, h, nw, w, d)
            bk = k.reshape(b, h, nw, w, d)
            bv = v.reshape(b, h, nw, w, d)

            def look(t):
                p = jnp.pad(t, ((0, 0), (0, 0), (1, 0), (0, 0), (0, 0)))
                return jnp.concatenate([p[:, :, :nw], p[:, :, 1:]], axis=3)
            bk2, bv2 = (look(bk), look(bv))
            seq = jnp.arange(n).reshape(nw, w)
            seq_p = jnp.pad(seq, ((1, 0), (0, 0)), constant_values=-1)
            jt = jnp.concatenate([seq_p[:nw], seq_p[1:]], axis=1)
            it = seq[:, :, None]
            jb = jt[:, None, :]
            mask = (it < jb) | (it > jb + w) | (jb == -1)
            sim = jnp.einsum('bhwie,bhwje->bhwij', bq, bk2) * QK_SCALE
            sim = jnp.where(mask, -jnp.finfo(sim.dtype).max, sim)
            attn = jax.nn.softmax(sim, -1)
            out = jnp.einsum('bhwij,bhwje->bhwie', attn, bv2)
            return out.reshape(b, h, n, d)

        def attn_layer(x, Wqkv, qs, ksc, Wo):
            b, n, _ = x.shape
            qkv = x @ Wqkv
            q, k, v = jnp.split(qkv, 3, -1)
            sh = lambda t: t.reshape(b, n, HEADS, DIM_HEAD).transpose(0, 2, 1, 3)
            q, k, v = (sh(q), sh(k), sh(v))
            q = l2norm(q) * qs
            k = l2norm(k) * ksc
            freqs, scale = rotary_tables(n)
            cos, sin = (jnp.cos(freqs), jnp.sin(freqs))
            q = q * cos * scale + rotate_half(q) * sin * scale
            inv = 1.0 / scale
            k = k * cos * inv + rotate_half(k) * sin * inv
            out = local_attention(q, k, v)
            out = out.transpose(0, 2, 1, 3).reshape(b, n, INNER)
            return out @ Wo

        def ffn_layer(x, g, bln, W1, b1, W2, b2):
            mu = x.mean(-1, keepdims=True)
            var = ((x - mu) ** 2).mean(-1, keepdims=True)
            xn = (x - mu) / jnp.sqrt(var + 1e-05) * g + bln
            hg = xn @ W1 + b1
            a, gate = jnp.split(hg, 2, -1)
            return a * jax.nn.gelu(gate, approximate=False) @ W2 + b2
        for i in range(DEPTH):
            x = attn_layer(shift_tokens(x), Wqkv[i], q_scale[i], k_scale[i], Wo[i]) + x
            x = ffn_layer(shift_tokens(x), ln_g[i], ln_b[i], W1[i], b1[i], W2[i], b2[i]) + x
        return x

    def _L1_attn_ref(x, w_q, w_k, w_v, w_o, b_o, ln_g, ln_b):
        import jax, jax.numpy as jnp
        import numpy as np
        D_MODEL = 128
        NUM_HEADS = 16
        D_K = D_MODEL // NUM_HEADS

        def _layer_norm(y, g, b, eps=1e-05):
            mu = jnp.mean(y, axis=-1, keepdims=True)
            var = jnp.var(y, axis=-1, keepdims=True)
            return (y - mu) * jax.lax.rsqrt(var + eps) * g + b
        B, S, D = x.shape

        def proj(w):
            return jnp.einsum('bsd,ed->bse', x, w).reshape(B, S, NUM_HEADS, D_K).transpose(0, 2, 1, 3)
        Q, K, V = (proj(w_q), proj(w_k), proj(w_v))
        scores = jnp.einsum('bhqd,bhkd->bhqk', Q, K) / jnp.sqrt(jnp.float32(D_K))
        attn = jax.nn.softmax(scores, axis=-1)
        out = jnp.einsum('bhqk,bhkd->bhqd', attn, V)
        out = out.transpose(0, 2, 1, 3).reshape(B, S, D)
        out = jnp.einsum('bsd,ed->bse', out, w_o) + b_o
        return _layer_norm(x + out, ln_g, ln_b)

    def _L1_ffn_ref(x, w_router, w_fc, w_proj):
        import jax, jax.numpy as jnp
        import numpy as np
        DIM = 128
        MLP_MULT = 4
        NUM_EXPERTS = 8
        EXPERT_HIDDEN = MLP_MULT * DIM // NUM_EXPERTS
        logits = jnp.einsum('bsd,ed->bse', jax.lax.stop_gradient(x), w_router)
        weights = jax.nn.softmax(logits, axis=-1)
        indices = jnp.argmax(weights, axis=-1)
        onehot = jax.nn.one_hot(indices, NUM_EXPERTS, dtype=x.dtype)
        h = jnp.einsum('bsd,ehd->bseh', x, w_fc)
        h = jnp.where(h >= 0, h, 0.5 * h)
        h = h * h
        out = jnp.einsum('bseh,edh,bse->bsd', h, w_proj, onehot)
        return out
    x = L0_attn_x
    x = x + 0.5 * _L0_ffn_ref(_layernorm(x, axis=-1), L0_ffn_Wqkv, L0_ffn_q_scale, L0_ffn_k_scale, L0_ffn_Wo, L0_ffn_ln_g, L0_ffn_ln_b, L0_ffn_W1, L0_ffn_b1, L0_ffn_W2, L0_ffn_b2)
    x = x + _L0_attn_ref(_layernorm(x, axis=-1), L0_attn_W_qkv, L0_attn_W_out, L0_attn_b_out)
    x = x + 0.5 * _L0_ffn_ref(_layernorm(x, axis=-1), L0_ffn_Wqkv, L0_ffn_q_scale, L0_ffn_k_scale, L0_ffn_Wo, L0_ffn_ln_g, L0_ffn_ln_b, L0_ffn_W1, L0_ffn_b1, L0_ffn_W2, L0_ffn_b2)
    x = x + 0.5 * _L1_ffn_ref(_layernorm(x, axis=-1), L1_ffn_w_router, L1_ffn_w_fc, L1_ffn_w_proj)
    x = x + _L1_attn_ref(_layernorm(x, axis=-1), L1_attn_w_q, L1_attn_w_k, L1_attn_w_v, L1_attn_w_o, L1_attn_b_o, L1_attn_ln_g, L1_attn_ln_b)
    x = x + 0.5 * _L1_ffn_ref(_layernorm(x, axis=-1), L1_ffn_w_router, L1_ffn_w_fc, L1_ffn_w_proj)
    return x

_drawn_inputs = setup_inputs


def setup_inputs(seed=0):
    import zlib

    import numpy as np

    out = dict(_drawn_inputs(seed))
    spreads = {'L0_ffn_q_scale': (1.0, 0.2),
     'L0_ffn_k_scale': (1.0, 0.2),
     'L0_ffn_ln_g': (1.0, 0.2),
     'L0_ffn_ln_b': (0.0, 0.326),
     'L0_ffn_b1': (0.0, 0.1),
     'L0_ffn_b2': (0.0, 0.1),
     'L1_attn_b_o': (0.0, 0.1),
     'L1_attn_ln_g': (1.0, 0.2),
     'L1_attn_ln_b': (0.0, 0.1)}
    factors = {}
    for name, (base, spread) in spreads.items():
        noise = np.random.default_rng([zlib.crc32(name.encode()), seed]).standard_normal(out[name].shape)
        drawn = base * np.exp(spread * noise) if base else spread * noise
        out[name] = jnp.asarray(drawn.astype(out[name].dtype))
    for name, factor in factors.items():
        out[name] = (out[name] * factor).astype(out[name].dtype)
    return out
```

```python
from contextlib import ExitStack

import concourse.bass as bass
from concourse import mybir

ALU = mybir.AluOpType
ACT = mybir.ActivationFunctionType
AX = mybir.AxisListType
F32 = mybir.dt.float32
F32R = mybir.dt.float32r
BF16 = mybir.dt.bfloat16

P = 128
D = 128
HALF = D // 2
BATCH = 2
SEQ = 1024
TPB = SEQ // P
TILES = BATCH * TPB
DEPTH = 6
HEADS = 16
DH = 64
RH = DH // 2
WIN = 32
INNER = HEADS * DH
KEYS = WIN + P
PADK = P - WIN
DI = int(D * 4 * 2 / 3)
FC = [(0, P), (P, P), (2 * P, DI - 2 * P)]
LAST = DI - 2 * P
SLOTS = 20
NEG = -1e35
LN_EPS = 1e-5
LIN_EPS = 1e-6
PAIRS = HEADS // 2
ORDER = [h for p0, p1 in ((0, 3), (3, 6), (6, 8)) for r in range(2) for h in range(2 * p0 + r, 2 * p1, 2)]
PLACE = [ORDER.index(h) for h in range(HEADS)]
SG = [(0, 3), (3, 6), (6, 9), (9, 12), (12, 14), (14, 16)]
NG = [(0, 6), (6, 12), (12, 16)]
NE = 8
EH = 64
H2 = 16
DK = D // H2
GQ = 4
NKB = SEQ // P


def slot(t):
    return t + 1 + (t >> 3)


STAGES = [("macaron", 0), ("linear", 0), ("macaron", 1), ("experts", 0), ("attention", 0), ("experts", 1)]


PARTS = dict(scores=6, maxima=6, exp_done=6, projected=6, proj_copied=6, p_turned=5, pT_ready=5, qk_turned=4,
             sine_part=4, normalised=3, inverted=3, cosine_part=2, turned_sum=2, squared=2, summed=2,
             qk_rotated=2, qT_ready=2, kT_ready=2, attended=2, aT_ready=2)


class Tiles:

    def __init__(self, done_before):
        self.done_before = done_before
        self.r = 0

    def tile(self, k):
        return self.r + k

    def done(self, k):
        return self.done_before + self.r + (k + 1)

    def part(self, k, name, i):
        return PARTS.get(name, 1) * (self.done(k) - 1) + (i + 1)


def run_steps(eng, tiles, step, rings=()):
    for k in (-1, 0, 1):
        step(k)
    with eng.Fori(0, TILES - 4, 2) as r:
        tiles.r = r
        step(2)
        step(3)
    tiles.r = 0
    for ring in rings:
        for bank in ring:
            ring[bank] = [(s, k + TILES - 6, i) for s, k, i in ring[bank]]
    for k in (14, 15, 16):
        step(k)


def build(nc, x_in, W, const, maskc, out):
    with ExitStack() as ctx:
        def sb(name, shape, dt=F32):
            return ctx.enter_context(nc.sbuf_tensor(name, shape, dt))

        sems = {}

        def sem(name):
            if name not in sems:
                sems[name] = ctx.enter_context(nc.semaphore(name))
            return sems[name]

        psum = ctx.enter_context(nc.psum_tensor("psum", [P, 8, 512], F32))
        bank = [psum[:, i, :] for i in range(8)]

        X = sb("X", [P, SLOTS, D])
        Y = sb("Y", [P, SLOTS, D])
        Z = sb("Z", [P, SLOTS, D])
        ident = sb("ident", [P, P])
        shift1 = sb("shift1", [P, P])
        lastrow = sb("lastrow", [P, P])
        keepk = sb("keepk", [P, TILES])
        rope = sb("rope", [P, 4, TPB, DH])
        identb = sb("identb", [P, P], BF16)
        mask = sb("mask", [P, TILES, KEYS], BF16)
        half = sb("half", [P, 32])
        eps = sb("eps", [P, TILES])
        waste = sb("waste", [P, 2])
        spare = sb("spare", [P, 1])
        wqkv = sb("wqkv", [P, 3 * INNER])
        wo = sb("wo", [P, PAIRS, D])
        w1 = sb("w1", [P, 2 * DI])
        w2 = sb("w2", [P, 3, D])
        lng = sb("lng", [P, 1])
        lnb = sb("lnb", [P, 1])
        b1 = sb("b1", [P, 6])
        qks = sb("qks", [P, 2, DH])
        ropes = sb("ropes", [P, 4, TPB, DH])
        ystage = sb("ystage", [P, D])
        xT = sb("xT", [P, P])
        raw = sb("raw", [P, 2, HEADS, DH])
        sq = sb("sq", [P, 2, HEADS, DH])
        rot = sb("rot", [P, 2, HEADS, DH])
        qkr = sb("qkr", [P, 2, HEADS, DH])
        ss = sb("ss", [P, 32])
        rn = sb("rn", [P, 32])
        qT = sb("qT", [P, PAIRS, P])
        kT = [sb(f"kT{i}", [P, PAIRS, KEYS]) for i in range(2)]
        V = [sb(f"V{i}", [P, INNER]) for i in range(2)]
        prob = sb("prob", [P, HEADS, 2 * P])
        nmax = sb("nmax", [P, HEADS])
        den = sb("den", [P, HEADS])
        rden = sb("rden", [P, HEADS])
        pTo = sb("pTo", [P, HEADS, P])
        pTp = sb("pTp", [P, HEADS, WIN])
        aT = sb("aT", [P, PAIRS, P])
        zstage = sb("zstage", [P, D])
        zn = sb("zn", [P, D])
        st6 = sb("st6", [P, 6])
        mv = sb("mv", [P, 2])
        rstd1 = sb("rstd1", [P, 2])
        xnT = sb("xnT", [P, TILES * P])
        gel = sb("gel", [P, 3, 512])
        gT = sb("gT", [P, 3, 512])
        masks = pTp[:, :, :].rearrange("p a b -> p (a b)")[:, 0:2 * KEYS]
        LOADS = 16 * 24
        mv8 = sb("mv8", [P, TPB, 2])
        rstd8 = sb("rstd8", [P, TPB])
        stt = sb("stt", [P, TILES, 6])
        mva = sb("mva", [P, TILES + 2, 2])
        rstda = sb("rstda", [P, TILES])
        wT = sb("wT", [P, 16, P])
        wrT = sb("wrT", [P, NE])
        bias = sb("bias", [P, 4, D])
        kvT = sb("kvT", [P, D])
        mixk = sb("mixk", [P, D + 1])
        ones = sb("ones", [P, 1])
        zden = sb("zden", [P, 4, 2])
        sel = sb("sel", [NE, 4, P])
        selb = sb("selb", [NE, 4, P], BF16)
        erank = sb("erank", [P, NE])
        lmax = sb("lmax", [P, 4])
        cand = sb("cand", [P, 4, NE])
        onehot = sb("onehot", [P, 4, NE])
        onehotT = sb("onehotT", [NE, 4, P], BF16)
        stackc = sb("stackc", [P, 4])
        wst = sb("wst", [P, 2, P])
        qst = sb("qst", [P, SEQ], F32R)
        kst = sb("kst", [P, SEQ], F32R)
        hi = V[0][:, :].bitcast(F32R)
        qtile = sb("qtile", [P, P], F32R)
        vg = V[1][:, :].rearrange("p (k r c) -> p k r c", k=NKB, r=GQ)
        oT = sb("oT", [P, P])
        orec = sb("orec", [P, GQ])
        amax = sb("amax", [P, GQ])

        phase = sem("phase_done")

        vector_engine = [None]

        def finish_phase(eng, n):
            eng.drain().then_inc(phase, 1)
            eng.wait_ge(phase, 4 * n)
            if eng is nc.vector or eng is vector_engine[0]:
                eng.memset(spare[:, :], 0.0)

        first_phase, n = [], 2
        for kind, _ in STAGES:
            first_phase.append(n)
            n += 2 + 2 * DEPTH if kind == "macaron" else 2
        END = n - 1
        macaron_at = [first_phase[i] for i, (kind, _) in enumerate(STAGES) if kind == "macaron"]

        def bc(ap, n):
            return ap.unsqueeze(2).broadcast_to([ap.shape[0], ap.shape[1], n])

        def rows(buf):
            return buf[:, 0:2 * (TPB + 1), :].rearrange("p (b s) f -> p b s f", b=BATCH)[:, :, 1:, :]

        def sync_program(sp):
            ld = sem("const_loaded")
            sp.dma_start(ident[:, :], const[:, 0:128]).then_inc(ld, 16)
            sp.dma_start(shift1[:, :], const[:, 128:256]).then_inc(ld, 16)
            sp.dma_start(lastrow[:, :], const[:, 256:384]).then_inc(ld, 16)
            sp.dma_start(keepk[:, :], const[:, 384:400]).then_inc(ld, 16)
            sp.dma_start(rope[:, :, :, :].rearrange("p a t d -> p (a t d)"),
                         const[:, 400:400 + 4 * TPB * DH]).then_inc(ld, 16)
            xv = x_in.rearrange("b (s p) f -> p (b s) f", p=P)
            sp.dma_start(X[:, 1:TPB + 1, :], xv[:, 0:TPB, :]).then_inc(ld, 16)
            sp.dma_start(X[:, TPB + 2:2 * TPB + 2, :], xv[:, TPB:, :]).then_inc(ld, 16)
            sp.dma_start(masks, maskc[:, 0:2 * KEYS]).then_inc(ld, 16)
            for i, (name, m) in enumerate((("L0_attn_W_qkv", 3), ("L0_attn_W_out", 1), ("L1_attn_w_q", 1),
                                           ("L1_attn_w_k", 1), ("L1_attn_w_v", 1), ("L1_attn_w_o", 1))):
                at = [0, 3, 4, 5, 6, 7][i]
                sp.dma_start(pTo[:, at:at + m, :], W[name].rearrange("(m p) d -> p m d", p=P)).then_inc(ld, 16)
            sp.dma_start(pTo[:, 8:12, :], W["L1_ffn_w_fc"].rearrange("(m e) h d -> (e h) m d", m=4)).then_inc(ld, 16)
            sp.dma_start(pTo[:, 12:16, :].rearrange("p m (e h) -> p (m e) h", e=2),
                         W["L1_ffn_w_proj"].rearrange("e d h -> d e h")).then_inc(ld, 16)
            sp.dma_start(ystage[0:NE, :], W["L1_ffn_w_router"]).then_inc(ld, 16)
            for i, name in enumerate(("L0_attn_b_out", "L1_attn_b_o", "L1_attn_ln_g", "L1_attn_ln_b")):
                sp.dma_start(bias[:, i, :], W[name].partition_broadcast(P)).then_inc(ld, 16)
            sp.dma_start(erank[:, :], maskc[:, 2 * KEYS:2 * KEYS + NE]).then_inc(ld, 16)
            sp.dma_start(stackc[:, :], maskc[:, 2 * KEYS + NE:2 * KEYS + NE + 4]).then_inc(ld, 16)
            sp.dma_start(sel[:, :, :].rearrange("p a b -> p (a b)"),
                         maskc[0:NE, 2 * KEYS + NE + 4:2 * KEYS + NE + 4 + 4 * P]).then_inc(ld, 16)
            for c in range(len(macaron_at)):
                with sp.Fori(0, DEPTH) as layer:
                    sp.wait_ge(phase, 4 * (macaron_at[c] - 1) + 8 * layer)
                    load_attention_weights(sp, c, layer)
                    sp.wait_ge(phase, 4 * macaron_at[c] + 8 * layer)
                    load_unit_weights(sp, c, layer)
            sp.wait_ge(phase, 4 * END)
            ov = out.rearrange("b (s p) f -> p (b s) f", p=P)
            sp.dma_start(ov[:, 0:TPB, :], X[:, 1:TPB + 1, :]).then_inc(sem("stored"), 16)
            sp.dma_start(ov[:, TPB:, :], X[:, TPB + 2:2 * TPB + 2, :]).then_inc(sem("stored"), 16)
            sp.wait_ge(sem("stored"), 32)

        AW = 4

        def load_attention_weights(sp, c, layer):
            s = sem("attn_weights")
            sp.dma_start(wqkv[:, :], W["Wqkv"][layer, :, :]).then_inc(s, 16)
            sp.dma_start(wo[:, :, :], W["Wo"][layer, :, :].rearrange("(c p) f -> p c f", p=P)).then_inc(s, 16)
            sp.dma_start(qks[:, 0, :], W["q_scale"][layer, :].partition_broadcast(P)).then_inc(s, 16)
            sp.dma_start(qks[:, 1, :], W["k_scale"][layer, :].partition_broadcast(P)).then_inc(s, 16)

        UW = 12

        def load_unit_weights(sp, c, layer):
            s = sem("unit_weights")
            sp.dma_start(w1[:, :], W["W1"][layer, :, :]).then_inc(s, 16)
            sp.dma_start(w2[:, 0:2, :], W["W2"][layer, 0:2 * P, :].rearrange("(c p) f -> p c f", p=P)).then_inc(s, 16)
            sp.dma_start(w2[0:LAST, 2, :], W["W2"][layer, 2 * P:DI, :]).then_inc(s, 16)
            sp.dma_start(w2[LAST:LAST + 1, 2, :], W["b2"][bass.ds(layer, 1), :]).then_inc(s, 16)
            sp.dma_start(lng[:, :], W["ln_g"][layer, :].unsqueeze(1)).then_inc(s, 16)
            sp.dma_start(lnb[:, :], W["ln_b"][layer, :].unsqueeze(1)).then_inc(s, 16)
            for h in range(2):
                for i, (c0, m) in enumerate(FC):
                    sp.dma_start(b1[0:m, 3 * h + i:3 * h + i + 1],
                                 W["b1"][layer, h * DI + c0:h * DI + c0 + m].unsqueeze(1)).then_inc(s, 16)

        def attention_pe(pe, c, layer):
            before = c * DEPTH * TILES + layer * TILES
            tl = Tiles(before)
            part = tl.part
            small, score, proj = {}, {}, {}

            def refill(ring, b, emptied_by):
                for s, k, i in ring.get(b, []):
                    pe.wait_ge(sem(s), part(k, s, i))
                ring[b] = emptied_by

            pe.wait_ge(sem("attn_weights"), 16 * AW * (c * DEPTH + 1) + 16 * AW * layer)

            def step(k):
                u, v = k + 1, k - 1
                has_u, has_t, has_v = u <= 15, 0 <= k <= 15, 0 <= v <= 15
                n, nu = tl.done(k), tl.done(u)
                refill(small, 0, [("input_staged", u, 0)] * has_u + [("unit_staged", v, 0)] * has_v)
                if has_u:
                    su = slot(tl.tile(u))
                    pe.matmul(bank[0][:, 0:HALF], shift1[:, :], Y[:, su, HALF:D], start=True, stop=False)
                    pe.matmul(bank[0][:, 0:HALF], lastrow[:, :], Y[:, su - 1, HALF:D],
                              start=False, stop=True).then_inc(sem("input_shifted"), 1)
                if has_v:
                    sv = slot(tl.tile(v))
                    pe.wait_ge(sem("attn_added"), tl.done(v))
                    pe.matmul(bank[0][:, HALF:D], shift1[:, :], Z[:, sv, HALF:D], start=True, stop=False)
                    pe.matmul(bank[0][:, HALF:D], lastrow[:, :], Z[:, sv - 1, HALF:D],
                              start=False, stop=True).then_inc(sem("unit_shifted"), 1)
                if has_t:
                    for w in range(2):
                        pe.wait_ge(sem("qk_rotated"), part(k, "qk_rotated", w))
                        for i in range(2):
                            b = (1 + 2 * w + i) % 3
                            refill(small, b, [("qT_ready" if w == 0 else "kT_ready", k, i)])
                            for j in range(4):
                                p = 4 * i + j
                                src = qkr[:, w, 2 * p:2 * p + 2, :].rearrange("p a d -> p (a d)")
                                mm = pe.transpose(bank[b][:, P * j:P * j + P], src, ident[:, :])
                            mm.then_inc(sem("qk_turned"), 1)
                if has_u:
                    refill(small, 2, [("xT_ready", u, 0)])
                    pe.wait_ge(sem("input_staged"), nu)
                    pe.transpose(bank[2][:, 0:P], ystage[:, :], ident[:, :]).then_inc(sem("x_turned"), 1)
                if has_t:
                    pe.wait_ge(sem("qT_ready"), part(k, "qT_ready", 1))
                    pe.wait_ge(sem("kT_ready"), part(k, "kT_ready", 1))
                    pe.wait_ge(sem("k_carried"), n)
                    for g, (h0, h1) in enumerate(SG):
                        b = 3 + g % 3
                        refill(score, b, [("exp_done", k, g)])
                        m = h1 - h0
                        pe.matmul(bank[b][:, 0:m * KEYS], identb[:, :],
                                  mask[:, tl.tile(k), :].unsqueeze(1).broadcast_to([P, m, KEYS]),
                                  start=True, stop=False, skip_group_check=True)
                        for i in range(m):
                            h = ORDER[h0 + i]
                            q0 = DH * (h % 2)
                            mm = pe.matmul(bank[b][:, i * KEYS:(i + 1) * KEYS], qT[q0:q0 + DH, h // 2, :],
                                           kT[k % 2][q0:q0 + DH, h // 2, :],
                                           start=False, stop=True, skip_group_check=True)
                        mm.then_inc(sem("scores"), 1)
                if has_v:
                    refill(small, 0, [("xnT_ready", v, 0)])
                    pe.wait_ge(sem("unit_normed"), tl.done(v))
                    pe.transpose(bank[0][:, 0:P], zn[:, :], ident[:, :]).then_inc(sem("unit_turned"), 1)
                if has_u:
                    pe.wait_ge(sem("xT_ready"), nu)
                    for q in range(4):
                        project(k, q)
                if has_t:
                    for g in range(4):
                        b = (7 + g) % 3
                        refill(small, b, [("pT_ready", k, g)])
                        pe.wait_ge(sem("normalised"), part(k, "normalised", [0, 1, 1, 2][g]))
                        if g == 3:
                            refill(small, 2, [("pT_ready", k, 4)])
                        for i in range(4):
                            mm = pe.transpose(bank[b][:, P * i:P * i + P], prob[:, 4 * g + i, P:2 * P], ident[:, :])
                        mm.then_inc(sem("p_turned"), 1)
                    for h in range(HEADS):
                        mm = pe.transpose(bank[2][:, WIN * h:WIN * h + WIN], prob[0:WIN, h, 0:P],
                                          ident[0:WIN, 0:WIN])
                    mm.then_inc(sem("p_turned"), 1)
                    pe.wait_ge(sem("v_ready"), n)
                    pe.wait_ge(sem("pT_ready"), part(k, "pT_ready", 4))
                    for e in range(2):
                        refill(small, e, [("aT_ready", k, e)])
                        for p in range(4 * e, 4 * e + 4):
                            for h in (2 * p, 2 * p + 1):
                                q0 = DH * (h % 2)
                                o = bank[e][q0:q0 + DH, P * (p % 4):P * (p % 4) + P]
                                pe.matmul(o, V[k % 2][:, DH * h:DH * h + DH], pTo[:, PLACE[h], :],
                                          start=True, stop=False, skip_group_check=True)
                                mm = pe.matmul(o[:, 0:WIN], V[1 - k % 2][:, DH * h:DH * h + DH],
                                               pTp[:, PLACE[h], :], start=False, stop=True,
                                               skip_group_check=True)
                        mm.then_inc(sem("attended"), 1)
                    refill(small, 2, [("attn_added", k, 0)])
                    pe.wait_ge(sem("aT_ready"), part(k, "aT_ready", 1))
                    for p in range(PAIRS):
                        mm = pe.matmul(bank[2][:, 0:D], aT[:, p, :], wo[:, p, :], start=(p == 0),
                                       stop=(p == PAIRS - 1))
                    mm.then_inc(sem("attn_out"), 1)
                if has_u:
                    project(k, 4)
                    project(k, 5)

            def project(k, q):
                b = 6 + q % 2
                refill(proj, b, [("proj_copied", k + 1, q)])
                pe.matmul(bank[b][:, :], xT[:, :], wqkv[:, 512 * q:512 * q + 512], start=True,
                          stop=True).then_inc(sem("projected"), 1)

            run_steps(pe, tl, step, (small, score, proj))

        def attention_act(act, c, layer):
            tl = Tiles(c * DEPTH * TILES + layer * TILES)
            part = tl.part
            act.wait_ge(sem("unit_weights"), 16 * UW * (c * DEPTH + 1) + 16 * UW * layer)

            def step(k):
                u, v = k + 1, k - 1
                has_u, has_t, has_v = u <= 15, 0 <= k <= 15, 0 <= v <= 15
                n, nu = tl.done(k), tl.done(u)
                if has_t:
                    for i in range(2):
                        act.wait_ge(sem("qk_turned"), part(k, "qk_turned", i))
                        act.activation(qT[:, 4 * i:4 * i + 4, :],
                                       bank[(1 + i) % 3][:, :].rearrange("p (a b) -> p a b", a=4),
                                       ACT.Copy).then_inc(sem("qT_ready"), 1)
                    for g, (h0, h1) in enumerate(SG):
                        act.wait_ge(sem("maxima"), part(k, "maxima", g))
                        for i, h in enumerate(range(h0, h1)):
                            e = act.activation(prob[:, h, PADK:2 * P],
                                               bank[3 + g % 3][:, i * KEYS:(i + 1) * KEYS], ACT.Exp,
                                               bias=nmax[:, h:h + 1], accum_out=den[:, h:h + 1])
                        e.then_inc(sem("exp_done"), 1)
                if has_v:
                    act.wait_ge(sem("unit_turned"), tl.done(v))
                    act.activation(xnT[:, bass.ts(tl.tile(v), P)], bank[0][:, 0:P], ACT.Identity,
                                   bias=lnb[:, 0:1], scale=lng[:, 0:1]).then_inc(sem("xnT_ready"), 1)
                if has_u:
                    for q in range(4):
                        act.wait_ge(sem("projected"), part(u, "projected", q))
                        act.activation(raw[:, q // 2, 8 * (q % 2):8 * (q % 2) + 8, :],
                                       bank[6 + q % 2][:, :].rearrange("p (a b) -> p a b", a=8),
                                       ACT.Copy).then_inc(sem("proj_copied"), 1)
                    for w in range(2):
                        act.wait_ge(sem("proj_copied"), part(u, "proj_copied", 2 * w + 1))
                        act.activation(sq[:, w, :, :], raw[:, w, :, :], ACT.Square).then_inc(
                            sem("squared"), 1)
                if has_t:
                    for g in range(4):
                        act.wait_ge(sem("p_turned"), part(k, "p_turned", g))
                        act.activation(pTo[:, 4 * g:4 * g + 4, :],
                                       bank[(7 + g) % 3][:, :].rearrange("p (a b) -> p a b", a=4),
                                       ACT.Copy).then_inc(sem("pT_ready"), 1)
                    act.wait_ge(sem("p_turned"), part(k, "p_turned", 4))
                    act.activation(pTp[:, :, :], bank[2][:, :].rearrange("p (a b) -> p a b", b=WIN),
                                   ACT.Copy).then_inc(sem("pT_ready"), 1)
                if has_u:
                    for q in (4, 5):
                        act.wait_ge(sem("projected"), part(u, "projected", q))
                        e = act.activation(V[u % 2][:, 512 * (q - 4):512 * (q - 3)], bank[6 + q % 2][:, :],
                                           ACT.Copy).then_inc(sem("proj_copied"), 1)
                    act.wait_ge(sem("proj_copied"), part(u, "proj_copied", 5))
                    act.nop().then_inc(sem("v_ready"), 1)

            run_steps(act, tl, step)

        def attention_dve(dve, c, layer):
            tl = Tiles(c * DEPTH * TILES + layer * TILES)
            part = tl.part
            dve.wait_ge(sem("attn_weights"), 16 * AW * (c * DEPTH + 1) + 16 * AW * layer)
            for w in range(2):
                for tr in range(2):
                    for i in range(2):
                        o = ropes[:, 2 * w + tr, :, RH * i:RH * i + RH]
                        s = qks[:, w, RH * (i ^ tr):RH * (i ^ tr) + RH].unsqueeze(1).broadcast_to([P, TPB, RH])
                        e = dve.tensor_tensor(o, rope[:, 2 * w + tr, :, RH * i:RH * i + RH], s, ALU.mult)
                        e.then_inc(sem("ropes_scaled"), 1)
            dve.wait_ge(sem("ropes_scaled"), 8 * (c * DEPTH + 1) + 8 * layer)

            def step(k):
                u, v = k + 1, k - 1
                has_u, has_t, has_v = u <= 15, 0 <= k <= 15, 0 <= v <= 15
                n, nu, nv = tl.done(k), tl.done(u), tl.done(v)
                if has_v:
                    dve.wait_ge(sem("unit_shifted"), nv)
                if has_u:
                    dve.wait_ge(sem("input_shifted"), nu)
                    dve.tensor_copy(ystage[:, HALF:D], bank[0][:, 0:HALF])
                    dve.tensor_copy(ystage[:, 0:HALF], Y[:, slot(tl.tile(u)), 0:HALF]).then_inc(
                        sem("input_staged"), 1)
                if has_v:
                    dve.tensor_copy(zstage[:, HALF:D], bank[0][:, HALF:D])
                    dve.tensor_copy(zstage[:, 0:HALF], Z[:, slot(tl.tile(v)), 0:HALF]).then_inc(
                        sem("unit_staged"), 1)
                    dve.wait_ge(sem("unit_staged"), nv)
                    dve.bn_stats(st6[:, :], zstage[:, :]).then_inc(sem("unit_stats"), 1)
                    dve.wait_ge(sem("unit_stats"), nv)
                    dve.memset(spare[:, :], 0.0)
                    dve.bn_aggr(mv[:, :], st6[:, :]).then_inc(sem("unit_moments"), 1)
                if has_t:
                    dve.tensor_scalar(kT[k % 2][:, :, 0:WIN], kT[1 - k % 2][:, :, P:KEYS],
                                      keepk[:, bass.ds(tl.tile(k), 1)], None, ALU.mult).then_inc(
                        sem("k_carried"), 1)
                    for i in range(2):
                        dve.wait_ge(sem("qk_turned"), part(k, "qk_turned", 2 + i))
                        dve.tensor_copy(kT[k % 2][:, 4 * i:4 * i + 4, WIN:KEYS],
                                        bank[(3 + i) % 3][:, :].rearrange("p (a b) -> p a b", a=4)).then_inc(
                            sem("kT_ready"), 1)
                if has_u:
                    dve.wait_ge(sem("x_turned"), nu)
                    dve.tensor_copy(xT[:, :], bank[2][:, 0:P]).then_inc(sem("xT_ready"), 1)
                if has_v:
                    dve.wait_ge(sem("unit_rstd"), nv)
                    dve.tensor_scalar(zn[:, :], zstage[:, :], mv[:, 0:1], rstd1[:, 1:2], ALU.subtract,
                                      ALU.mult).then_inc(sem("unit_normed"), 1)
                if has_t:
                    def maxima(g):
                        h0, h1 = SG[g]
                        dve.wait_ge(sem("scores"), part(k, "scores", g))
                        dve.tensor_reduce(nmax[:, h0:h1],
                                          bank[3 + g % 3][:, 0:(h1 - h0) * KEYS].rearrange(
                                              "p (a b) -> p a b", b=KEYS),
                                          AX.X, ALU.max, negate=True).then_inc(sem("maxima"), 1)

                    def invert(j):
                        h0, h1 = NG[j]
                        dve.wait_ge(sem("exp_done"), part(k, "exp_done", 2 * j + 1))
                        dve.reciprocal(rden[:, h0:h1], den[:, h0:h1]).then_inc(sem("inverted"), 1)

                    for g in range(4):
                        maxima(g)
                    invert(0)
                    maxima(4)
                    maxima(5)
                    invert(1)
                    invert(2)
                if has_u:
                    ti = tl.tile(u) & 7
                    for w in range(2):
                        dve.wait_ge(sem("squared"), part(u, "squared", w))
                        dve.tensor_reduce(ss[:, 16 * w:16 * w + 16], sq[:, w, :, :], AX.X, ALU.add).then_inc(
                            sem("summed"), 1)
                    dve.wait_ge(sem("summed"), part(u, "summed", 1))
                    dve.tensor_scalar(ss[:, :], ss[:, :], 1e-24, None, ALU.max).then_inc(sem("norms_squared"), 1)
                    for w in range(2):
                        for i in range(2):
                            dve.tensor_tensor(sq[:, w, :, RH * i:RH * i + RH],
                                              raw[:, w, :, RH * (1 - i):RH * (1 - i) + RH],
                                              ropes[:, 2 * w + 1, bass.ds(ti, 1), RH * i:RH * i + RH].broadcast_to(
                                                  [P, HEADS, RH]), ALU.mult).then_inc(
                                sem("sine_part"), 1)
                    for w in range(2):
                        dve.wait_ge(sem("cosine_part"), part(u, "cosine_part", w))
                        dve.wait_ge(sem("sine_part"), part(u, "sine_part", 2 * w + 1))
                        dve.tensor_tensor(rot[:, w, :, :], rot[:, w, :, :], sq[:, w, :, :], ALU.add).then_inc(
                            sem("turned_sum"), 1)
                if has_t:
                    for e in range(2):
                        dve.wait_ge(sem("attended"), part(k, "attended", e))
                        dve.tensor_copy(aT[:, 4 * e:4 * e + 4, :],
                                        bank[e][:, :].rearrange("p (a b) -> p a b", a=4)).then_inc(
                            sem("aT_ready"), 1)
                if has_u:
                    dve.wait_ge(sem("rnorm"), nu)
                    for w in range(2):
                        dve.wait_ge(sem("turned_sum"), part(u, "turned_sum", w))
                        dve.tensor_tensor(qkr[:, w, :, :], rot[:, w, :, :], bc(rn[:, 16 * w:16 * w + 16], DH),
                                          ALU.mult).then_inc(sem("qk_rotated"), 1)
                        if w == 0 and has_t:
                            add_out(k)
                elif has_t:
                    add_out(k)

            def add_out(k):
                dve.wait_ge(sem("attn_out"), tl.done(k))
                s = slot(tl.tile(k))
                dve.tensor_tensor(Z[:, s, :], bank[2][:, 0:D], Y[:, s, :], ALU.add).then_inc(
                    sem("attn_added"), 1)

            run_steps(dve, tl, step)

        def attention_pool(pool, c, layer):
            tl = Tiles(c * DEPTH * TILES + layer * TILES)
            part = tl.part
            pool.wait_ge(sem("ropes_scaled"), 8 * (c * DEPTH + 1) + 8 * layer)

            def step(k):
                u, v = k + 1, k - 1
                has_u, has_t, has_v = u <= 15, 0 <= k <= 15, 0 <= v <= 15
                n, nu, nv = tl.done(k), tl.done(u), tl.done(v)
                if has_v:
                    pool.wait_ge(sem("unit_moments"), nv)
                    pool.tensor_tensor(rstd1[:, 0:1], mv[:, 1:2], eps[:, 0:1], ALU.add).then_inc(
                        sem("unit_var"), 1)
                    pool.wait_ge(sem("unit_var"), nv)
                    pool.tensor_tensor(rstd1[:, 1:2], rstd1[:, 0:1], half[:, 0:1], ALU.pow).then_inc(
                        sem("unit_rstd"), 1)
                if has_t:
                    for j, (h0, h1) in enumerate(NG):
                        pool.wait_ge(sem("inverted"), part(k, "inverted", j))
                        pool.tensor_tensor(prob[:, h0:h1, PADK:2 * P], prob[:, h0:h1, PADK:2 * P],
                                           bc(rden[:, h0:h1], KEYS), ALU.mult).then_inc(
                            sem("normalised"), 1)
                if has_u:
                    ti = tl.tile(u) & 7
                    for w in range(2):
                        pool.wait_ge(sem("proj_copied"), part(u, "proj_copied", 2 * w + 1))
                        pool.tensor_tensor(rot[:, w, :, :], raw[:, w, :, :],
                                           ropes[:, 2 * w, bass.ds(ti, 1), :].broadcast_to([P, HEADS, DH]),
                                           ALU.mult).then_inc(sem("cosine_part"), 1)
                    pool.wait_ge(sem("norms_squared"), nu)
                    pool.tensor_tensor(rn[:, :], ss[:, :], half[:, :], ALU.pow).then_inc(sem("rnorm"), 1)

            run_steps(pool, tl, step)

        def unit_counts(c, layer, j):
            return c * DEPTH * 4 + layer * 4 + j + 1

        def unit_pe(pe, c, layer):
            pe.wait_ge(sem("unit_weights"), 16 * UW * (c * DEPTH + 1) + 16 * UW * layer)

            def group(j, first):
                n = unit_counts(c, layer, j)
                x = xnT[:, bass.ts(j, 512)]
                for i, (c0, m) in enumerate(FC):
                    for h in (1, 0):
                        pe.matmul(bank[3 * h + i][0:m, :], w1[:, h * DI + c0:h * DI + c0 + m], x,
                                  start=True, stop=True).then_inc(sem("unit_h"), 1)
                if not first:
                    pe.wait_ge(sem("unit_added"), n - 1)
                for i in range(3):
                    m = P if i < 2 else LAST + 1
                    pe.wait_ge(sem("gated"), 3 * (n - 1) + i + 1)
                    for q in range(4):
                        mm = pe.matmul(bank[6][:, P * q:P * q + P], gT[0:m, i, P * q:P * q + P], w2[0:m, i, :],
                                       start=(i == 0 and q == 0), stop=(i == 2), skip_group_check=True)
                mm.then_inc(sem("unit_out"), 1)

            group(0, True)
            with pe.Fori(1, 4) as j:
                group(j, False)

        def unit_act(act, c, layer):
            with act.Fori(0, 4) as j:
                n = unit_counts(c, layer, j)
                for i, (_, m) in enumerate(FC):
                    act.wait_ge(sem("unit_h"), 6 * (n - 1) + 2 * i + 1)
                    act.activation(gel[0:m, i, :], bank[3 + i][0:m, :], ACT.Gelu,
                                   bias=b1[0:m, 3 + i:4 + i]).then_inc(sem("gelu"), 1)

        def unit_dve(dve, c, layer):
            with dve.Fori(0, 4) as j:
                n = unit_counts(c, layer, j)
                for i, (_, m) in enumerate(FC):
                    dve.wait_ge(sem("unit_h"), 6 * (n - 1) + 2 * i + 2)
                    dve.wait_ge(sem("gelu"), 3 * (n - 1) + i + 1)
                    dve.scalar_tensor_tensor(gT[0:m, i, :], bank[i][0:m, :], b1[0:m, i:i + 1],
                                             gel[0:m, i, :], ALU.add, ALU.mult).then_inc(
                        sem("gated"), 1)
                dve.wait_ge(sem("unit_out"), n)
                s = 4 * j + 1 + (j >> 1)
                dve.tensor_tensor(Y[:, bass.ds(s, 4), :], bank[6][:, :].rearrange("p (a b) -> p a b", a=4),
                                  Z[:, bass.ds(s, 4), :], ALU.add).then_inc(sem("unit_added"), 1)

        def stats_dve(dve, n):
            with dve.Fori(0, TILES) as t:
                dve.bn_stats(stt[:, bass.ds(t, 1), :].rearrange("p a b -> p (a b)"),
                             X[:, bass.ds(slot(t), 1), :].rearrange("p a b -> p (a b)")).then_inc(
                    sem("x_stats"), 1)
            dve.wait_ge(sem("x_stats"), TILES * n)
            for t in range(TILES):
                dve.bn_aggr(mva[:, t, :], stt[:, t, :]).then_inc(sem("x_moments"), 1)

        def stats_pool(pool, n):
            pool.wait_ge(sem("x_moments"), TILES * n)
            pool.tensor_tensor(rstda[:, :], mva[:, 0:TILES, 1], eps[:, :], ALU.add).then_inc(sem("x_var"), 1)
            pool.wait_ge(sem("x_var"), n)
            pool.tensor_tensor(rstda[:, :], rstda[:, :], half[:, 0:TILES], ALU.pow).then_inc(sem("x_rstd"), 1)

        def norm_dve(dve, n):
            dve.wait_ge(sem("x_rstd"), n)
            with dve.Fori(0, TILES) as t:
                dve.tensor_scalar(Y[:, bass.ds(slot(t), 1), :].rearrange("p a b -> p (a b)"),
                                  X[:, bass.ds(slot(t), 1), :].rearrange("p a b -> p (a b)"),
                                  mva[:, bass.ds(t, 1), 0:1].rearrange("p a b -> p (a b)"),
                                  rstda[:, bass.ds(t, 1)], ALU.subtract, ALU.mult)

        def norm_tiles_dve(dve, out8, batch, done):
            for i in range(TPB):
                t = TPB * batch + i
                dve.tensor_scalar(out8[:, i, :], X[:, bass.ds((TPB + 1) * batch + 1 + i, 1), :].rearrange(
                    "p a f -> p (a f)"),
                    mva[:, bass.ds(t, 1), 0:1].rearrange("p a b -> p (a b)"), rstda[:, bass.ds(t, 1)],
                    ALU.subtract, ALU.mult).then_inc(sem(done), 1)

        stage8 = aT
        yT8 = qT

        def turn8_pe(pe, name, n8, n):
            for h in range(2):
                pe.wait_ge(sem(name + "_normed"), n8)
                for i in range(4):
                    mm = pe.transpose(bank[h][:, P * i:P * i + P], stage8[:, 4 * h + i, :], ident[:, :])
                mm.then_inc(sem(name + "_turned%d" % h), 1)

        def turn8_act(act, name, n):
            for h in range(2):
                act.wait_ge(sem(name + "_turned%d" % h), n)
                act.activation(yT8[:, 4 * h:4 * h + 4, :], bank[h][:, :].rearrange("p (a b) -> p a b", a=4),
                               ACT.Copy).then_inc(sem(name + "_yT%d" % h), 1)

        def flat8(buf):
            return buf[:, :, :].rearrange("p a b -> p (a b)")

        lin_q = flat8(raw[:, 0, :, :])
        lin_k = raw[:, 1, :, :].rearrange("p h d -> p (h d)").rearrange("p (t f) -> p t f", f=D)
        lin_v = sq[:, 0, :, :].rearrange("p h d -> p (h d)").rearrange("p (t f) -> p t f", f=D)

        def linear_pe(pe):
            with pe.Fori(0, BATCH) as b:
                n = b + 1
                turn8_pe(pe, "lin", TPB * n, n)
                pe.wait_ge(sem("lin_yT0"), n)
                pe.wait_ge(sem("lin_yT1"), n)
                for h in range(2):
                    pe.matmul(bank[2 + h][:, :], wT[:, 0, :], flat8(yT8)[:, 512 * h:512 * h + 512], start=True,
                              stop=True).then_inc(sem("lin_q%d" % h), 1)
                for i in range(TPB):
                    mm = pe.matmul(bank[4 + i // 2][:, 256 * (i % 2):256 * (i % 2) + 256], yT8[:, i, :],
                                   wT[:, 1:3, :].rearrange("p a b -> p (a b)"), start=True, stop=True)
                    if i % 2:
                        mm.then_inc(sem("lin_kv"), 1)
                pe.wait_ge(sem("lin_kv_kept"), n)
                for i in range(TPB):
                    mm = pe.matmul(bank[0][:, 0:D], lin_v[:, i, :], lin_k[:, i, :], start=(i == 0),
                                   stop=(i == TPB - 1))
                mm.then_inc(sem("lin_state"), 1)
                for i in range(TPB):
                    mm = pe.matmul(bank[1][:, 0:1], lin_k[:, i, :], ones[:, :], start=(i == 0),
                                   stop=(i == TPB - 1))
                mm.then_inc(sem("lin_ksum"), 1)
                pe.wait_ge(sem("lin_state_kept"), n)
                pe.matmul(bank[2][:, 0:D], kvT[:, :], wT[:, 3, :], start=True, stop=True).then_inc(
                    sem("lin_mixed"), 1)
                pe.wait_ge(sem("lin_mix_kept"), n)
                for i in range(TPB):
                    mm = pe.matmul(bank[4 + i // 2][:, 256 * (i % 2):256 * (i % 2) + D + 1],
                                   lin_q[:, P * i:P * i + P], mixk[:, :], start=True, stop=True)
                    if i % 2:
                        mm.then_inc(sem("lin_out"), 1)

        def linear_act(act):
            with act.Fori(0, BATCH) as b:
                turn8_act(act, "lin", b + 1)

        def linear_dve(dve):
            with dve.Fori(0, BATCH) as b:
                n = b + 1
                norm_tiles_dve(dve, stage8, b, "lin_normed")
                for h in range(2):
                    dve.wait_ge(sem("lin_q%d" % h), n)
                    dve.tensor_scalar(lin_q[:, 512 * h:512 * h + 512], bank[2 + h][:, :], 0.0, LIN_EPS,
                                      ALU.max, ALU.add).then_inc(sem("lin_q_kept"), 1)
                for i in range(4):
                    dve.wait_ge(sem("lin_kv"), 4 * (n - 1) + i + 1)
                    src = bank[4 + i][:, :].rearrange("p (t a f) -> p t a f", t=2, a=2)
                    dve.tensor_scalar(lin_k[:, 2 * i:2 * i + 2, :], src[:, :, 0, :], 0.0, LIN_EPS, ALU.max, ALU.add)
                    e = dve.tensor_copy(lin_v[:, 2 * i:2 * i + 2, :], src[:, :, 1, :])
                e.then_inc(sem("lin_kv_kept"), 1)
                dve.wait_ge(sem("lin_state"), n)
                dve.tensor_copy(kvT[:, :], bank[0][:, 0:D]).then_inc(sem("lin_state_kept"), 1)
                dve.wait_ge(sem("lin_ksum"), n)
                dve.tensor_copy(mixk[:, D:D + 1], bank[1][:, 0:1])
                dve.wait_ge(sem("lin_mixed"), n)
                dve.tensor_copy(mixk[:, 0:D], bank[2][:, 0:D]).then_inc(sem("lin_mix_kept"), 1)
                for i in range(4):
                    dve.wait_ge(sem("lin_out"), 4 * (n - 1) + i + 1)
                    src = bank[4 + i][:, :].rearrange("p (t f) -> p t f", t=2)
                    dve.tensor_scalar(zden[:, i, :], src[:, :, D], LIN_EPS, None, ALU.add).then_inc(
                        sem("lin_den"), 1)
                    dve.wait_ge(sem("lin_den"), 4 * b + i + 1)
                    dve.reciprocal(zden[:, i, :], zden[:, i, :]).then_inc(sem("lin_inv"), 1)
                    dve.wait_ge(sem("lin_inv"), 4 * b + i + 1)
                    for j in range(2):
                        xs = X[:, bass.ds((TPB + 1) * b + 1 + 2 * i + j, 1), :].rearrange("p a f -> p (a f)")
                        e = dve.scalar_tensor_tensor(xs, src[:, j, 0:D], zden[:, i, j:j + 1], xs, ALU.mult,
                                                     ALU.add).then_inc(sem("lin_added"), 1)
                dve.wait_ge(sem("lin_added"), TPB * n)
                xs = X[:, bass.ds((TPB + 1) * b + 1, TPB), :]
                dve.tensor_tensor(xs, xs, bias[:, 0, :].unsqueeze(1).broadcast_to([P, TPB, D]), ALU.add)

        ex_y = stage8[:, 0:4, :]
        ex_yT = yT8[:, 0:4, :]
        ex_h = raw[:, :, :, :].rearrange("p a h d -> p (a h d)").rearrange("p (m t) -> p m t", m=4)
        ex_g = sq[:, :, :, :].rearrange("p a h d -> p (a h d)").rearrange("p (m t) -> p m t", m=4)
        ex_g2 = rot[:, :, :, :].rearrange("p a h d -> p (a h d)").rearrange("p (m t) -> p m t", m=4)

        def experts_pe(pe, c):
            with pe.Fori(0, 4) as j:
                n = 4 * c + j + 1
                pe.wait_ge(sem("ex_normed"), 4 * n)
                for i in range(4):
                    mm = pe.transpose(bank[0][:, P * i:P * i + P], ex_y[:, i, :], ident[:, :])
                mm.then_inc(sem("ex_turned"), 1)
                pe.wait_ge(sem("ex_yT"), n)
                for i in range(4):
                    mm = pe.matmul(bank[1][:, NE * i:NE * i + NE], ex_yT[:, i, :], wrT[:, :], start=True, stop=True)
                mm.then_inc(sem("ex_logits"), 1)
                for m in range(4):
                    if m >= 2:
                        pe.wait_ge(sem("ex_leaky"), 4 * (n - 1) + (m - 2) + 1)
                    pe.matmul(bank[3 + m % 2][:, :], wT[:, 8 + m, :], ex_yT.rearrange("p a b -> p (a b)"),
                              start=True, stop=True).then_inc(sem("ex_fc"), 1)
                pe.wait_ge(sem("ex_onehot"), n)
                for i in range(4):
                    mm = pe.transpose(bank[2][0:NE, P * i:P * i + P], onehot[:, i, :], ident[:, :])
                mm.then_inc(sem("ex_onehot_turned"), 1)
                pe.wait_ge(sem("ex_onehotT"), n)
                for m in range(4):
                    if m >= 2:
                        pe.wait_ge(sem("ex_gated"), 4 * (n - 1) + (m - 2) + 1)
                    pe.matmul(bank[5 + m % 2][:, :], selb[:, m, :], onehotT[:, :, :].rearrange("p a b -> p (a b)"),
                              start=True, stop=True).then_inc(sem("ex_gate"), 1)
                for m in range(4):
                    pe.wait_ge(sem("ex_squared"), 4 * (n - 1) + m + 1)
                    for i in range(4):
                        mm = pe.matmul(bank[7][:, P * i:P * i + P], ex_g2[:, m, P * i:P * i + P],
                                       wT[:, 12 + m, :], start=(m == 0 and i == 0), stop=(m == 3),
                                       skip_group_check=True)
                mm.then_inc(sem("ex_out"), 1)

        def experts_act(act, c):
            with act.Fori(0, 4) as j:
                n = 4 * c + j + 1
                act.wait_ge(sem("ex_turned"), n)
                act.activation(ex_yT, bank[0][:, :].rearrange("p (a b) -> p a b", a=4), ACT.Copy).then_inc(
                    sem("ex_yT"), 1)
                for m in range(4):
                    act.wait_ge(sem("ex_fc"), 4 * (n - 1) + m + 1)
                    act.activation(ex_h[:, m, :], bank[3 + m % 2][:, :], ACT.Copy, scale=0.5).then_inc(
                        sem("ex_halved"), 1)
                for m in range(4):
                    act.wait_ge(sem("ex_gated"), 4 * (n - 1) + m + 1)
                    act.activation(ex_g2[:, m, :], ex_g[:, m, :], ACT.Square).then_inc(
                        sem("ex_squared"), 1)

        def experts_dve(dve, c):
            with dve.Fori(0, 4) as j:
                n = 4 * c + j + 1
                s = 4 * j + 1 + (j >> 1)
                for i in range(4):
                    dve.tensor_scalar(ex_y[:, i, :], X[:, bass.ds(s + i, 1), :].rearrange("p a f -> p (a f)"),
                                      mva[:, bass.ds(4 * j + i, 1), 0:1].rearrange("p a b -> p (a b)"),
                                      rstda[:, bass.ds(4 * j + i, 1)], ALU.subtract, ALU.mult).then_inc(
                        sem("ex_normed"), 1)
                logits = bank[1][:, 0:4 * NE].rearrange("p (a e) -> p a e", e=NE)
                dve.wait_ge(sem("ex_logits"), n)
                dve.tensor_reduce(lmax[:, :], logits, AX.X, ALU.max).then_inc(sem("ex_lmax"), 1)
                dve.wait_ge(sem("ex_lmax"), n)
                dve.tensor_tensor(cand[:, :, :], logits, bc(lmax[:, :], NE), ALU.is_ge).then_inc(
                    sem("ex_tied"), 1)
                dve.wait_ge(sem("ex_tied"), n)
                dve.tensor_tensor(cand[:, :, :], cand[:, :, :],
                                  erank[:, :].unsqueeze(1).broadcast_to([P, 4, NE]), ALU.mult).then_inc(
                    sem("ex_ranked"), 1)
                dve.wait_ge(sem("ex_ranked"), n)
                dve.tensor_reduce(lmax[:, :], cand[:, :, :], AX.X, ALU.max).then_inc(sem("ex_first"), 1)
                dve.wait_ge(sem("ex_first"), n)
                dve.tensor_tensor(onehot[:, :, :], cand[:, :, :], bc(lmax[:, :], NE), ALU.is_equal).then_inc(
                    sem("ex_onehot"), 1)
                for m in range(4):
                    dve.wait_ge(sem("ex_halved"), 4 * (n - 1) + m + 1)
                    dve.tensor_tensor(ex_h[:, m, :], bank[3 + m % 2][:, :], ex_h[:, m, :], ALU.max).then_inc(
                        sem("ex_leaky"), 1)
                dve.wait_ge(sem("ex_onehot_turned"), n)
                dve.tensor_copy(onehotT[:, :, :], bank[2][0:NE, :].rearrange("p (a b) -> p a b", a=4)).then_inc(
                    sem("ex_onehotT"), 1)
                for m in range(4):
                    dve.wait_ge(sem("ex_leaky"), 4 * (n - 1) + m + 1)
                    dve.wait_ge(sem("ex_gate"), 4 * (n - 1) + m + 1)
                    dve.tensor_tensor(ex_g[:, m, :], bank[5 + m % 2][:, :], ex_h[:, m, :], ALU.mult).then_inc(
                        sem("ex_gated"), 1)
                dve.wait_ge(sem("ex_out"), n)
                xs = X[:, bass.ds(s, 4), :]
                dve.scalar_tensor_tensor(xs, bank[7][:, :].rearrange("p (a b) -> p a b", a=4), 0.5, xs,
                                         ALU.mult, ALU.add)

        at_v = kT[0][:, :, 0:P]
        at_q = raw[:, 0, :, :].rearrange("p h d -> p (h d)")
        at_k = raw[:, 1, :, :].rearrange("p h d -> p (h d)")
        at_p = prob[:, :, :].rearrange("p a b -> p (a b)").rearrange("p (r k) -> p r k", r=GQ)
        at_pT = [b[:, :, :, :].rearrange("p a h d -> p (a h d)").rearrange("p (k r q) -> p k r q", k=4, r=GQ)
                 for b in (rot, qkr)]
        at_o = kT[1][:, :, 0:P]
        at_oT = pTo[:, 0:8, :]
        UNITS = 4 * TPB

        def attention2_pe(pe):
            with pe.Fori(0, BATCH) as b:
                turn8_pe(pe, "at", TPB * (b + 1), b + 1)
                pe.wait_ge(sem("at_yT0"), b + 1)
                pe.wait_ge(sem("at_yT1"), b + 1)
                for h in range(2):
                    for i in range(4):
                        mm = pe.matmul(bank[2 + h][:, P * i:P * i + P], yT8[:, 4 * h + i, :], wT[:, 6, :],
                                       start=True, stop=True)
                    mm.then_inc(sem("at_v%d" % h), 1)
                with pe.Fori(0, 4) as g:
                    ng = 4 * b + g + 1
                    for w in range(2):
                        pe.wait_ge(sem("at_weights%d" % w), ng)
                        for h in range(2):
                            pe.matmul(bank[4 + 2 * w + h][:, :], wst[:, w, :], flat8(yT8)[:, 512 * h:512 * h + 512],
                                      start=True, stop=True).then_inc(sem("at_proj"), 1)
                    with pe.Fori(0, TPB) as t:
                        pe.wait_ge(sem("at_stacked1"), ng)
                        pe.wait_ge(sem("at_values"), ng)
                        n = UNITS * b + TPB * g + t + 1
                        pe.wait_ge(sem("at_qtile"), n)
                        for r in range(GQ):
                            scores2(pe, n, r)
                            if r:
                                turn_p2(pe, n, r - 1)
                        turn_p2(pe, n, GQ - 1)
                        pe.wait_ge(sem("at_pT_a"), 4 * n)
                        pe.wait_ge(sem("at_pT_b"), 4 * n)
                        for kb in range(NKB):
                            for r in range(GQ):
                                mm = pe.matmul(bank[6][32 * r:32 * r + 32, 0:P], vg[:, kb, r, :],
                                               at_pT[kb // 4][:, kb % 4, r, :], start=(kb == 0),
                                               stop=(kb == NKB - 1), skip_group_check=True)
                        mm.then_inc(sem("at_attended"), 1)
                        pe.wait_ge(sem("at_oT"), n)
                        pe.transpose(bank[7][:, 0:P], oT[:, :], ident[:, :]).then_inc(sem("at_o_turned"), 1)
                pe.wait_ge(sem("at_o"), UNITS * (b + 1))
                for h in range(2):
                    for i in range(4):
                        mm = pe.transpose(bank[h][:, P * i:P * i + P], at_o[:, 4 * h + i, :], ident[:, :])
                    mm.then_inc(sem("at_all_turned%d" % h), 1)
                for h in range(2):
                    pe.wait_ge(sem("at_all_oT%d" % h), b + 1)
                    for i in range(4):
                        mm = pe.matmul(bank[2 + h][:, P * i:P * i + P], at_oT[:, 4 * h + i, :], wT[:, 7, :],
                                       start=True, stop=True)
                    mm.then_inc(sem("at_out%d" % h), 1)

        def scores2(pe, n, r):
            for h in range(2):
                if r >= 2:
                    pe.wait_ge(sem("at_exp"), 4 * (n - 1) + (r - 2) + 1)
                mm = pe.matmul(bank[2 * (r % 2) + h][:, :], qtile[32 * r:32 * r + 32, :],
                               kst[32 * r:32 * r + 32, 512 * h:512 * h + 512], start=True, stop=True)
            mm.then_inc(sem("at_scores"), 1)

        def turn_p2(pe, n, r):
            for h in range(2):
                if r >= 1:
                    pe.wait_ge(sem("at_pT_" + "ab"[h]), 4 * (n - 1) + r)
                pe.wait_ge(sem("at_exp"), 4 * (n - 1) + r + 1)
                for i in range(4):
                    mm = pe.transpose(bank[4 + h][:, P * i:P * i + P], at_p[:, r, 512 * h + P * i:512 * h + P * i + P],
                                      ident[:, :])
                mm.then_inc(sem("at_p_turned" + "ab"[h]), 1)

        def attention2_act(act):
            with act.Fori(0, BATCH) as b:
                turn8_act(act, "at", b + 1)
                with act.Fori(0, 4) as g:
                    ng = 4 * b + g + 1
                    for w in range(2):
                        for h in range(2):
                            act.wait_ge(sem("at_proj"), 4 * (ng - 1) + 2 * w + h + 1)
                            act.activation((at_q, at_k)[w][:, 512 * h:512 * h + 512], bank[4 + 2 * w + h][:, :],
                                           ACT.Copy, scale=(float(DK) ** -0.5, 1.0)[w]).then_inc(
                                sem("at_proj_copied%d" % w), 1)
                    with act.Fori(0, TPB) as t:
                        n = UNITS * b + TPB * g + t + 1
                        for r in range(GQ):
                            act.wait_ge(sem("at_maxima"), 4 * (n - 1) + r + 1)
                            act.activation(at_p[:, r, :], psum[:, 2 * (r % 2):2 * (r % 2) + 2, :].rearrange(
                                "p a b -> p (a b)"), ACT.Exp, bias=amax[:, r:r + 1]).then_inc(
                                sem("at_exp"), 1)
                            if r:
                                keep_pT_act(act, n, r - 1)
                        keep_pT_act(act, n, GQ - 1)
                        act.wait_ge(sem("at_attended"), n)
                        act.activation(oT[:, :], bank[6][:, 0:P], ACT.Copy).then_inc(sem("at_oT"), 1)
                for h in range(2):
                    act.wait_ge(sem("at_all_turned%d" % h), b + 1)
                    act.activation(at_oT[:, 4 * h:4 * h + 4, :], bank[h][:, :].rearrange("p (a b) -> p a b", a=4),
                                   ACT.Copy).then_inc(sem("at_all_oT%d" % h), 1)

        def keep_pT_act(act, n, r):
            act.wait_ge(sem("at_p_turneda"), 4 * (n - 1) + r + 1)
            act.activation(at_pT[0][:, :, r, :], bank[4][:, :].rearrange("p (a b) -> p a b", a=4),
                           ACT.Copy).then_inc(sem("at_pT_a"), 1)

        def attention2_dve(dve):
            dve.memset(V[1][:, :], 0.0).then_inc(sem("at_zeroed"), 1)
            dve.wait_ge(sem("at_zeroed"), 1)
            dve.memset(vg[:, :, :, DK:DK + 1], 1.0)
            with dve.Fori(0, BATCH) as b:
                norm_tiles_dve(dve, stage8, b, "at_normed")
                for h in range(2):
                    dve.wait_ge(sem("at_v%d" % h), b + 1)
                    dve.tensor_copy(at_v[:, 4 * h:4 * h + 4, :],
                                    bank[2 + h][:, :].rearrange("p (a b) -> p a b", a=4)).then_inc(
                        sem("at_v_kept"), 1)
                with dve.Fori(0, 4) as g:
                    ng = 4 * b + g + 1
                    for w in range(2):
                        src = wT[:, 4 + w, bass.ds(32 * g, 32)].rearrange("p (r d) -> p r d", d=DK)
                        for cpy in range(4):
                            e = dve.tensor_copy(
                                wst[:, w, :].rearrange("p (r c d) -> p r c d", r=GQ, c=4)[:, :, cpy, :], src)
                        e.then_inc(sem("at_weights%d" % w), 1)
                    dve.wait_ge(sem("at_v_kept"), 2 * (b + 1))
                    for r in range(GQ):
                        e = dve.tensor_scalar(vg[:, :, r, 0:DK], at_v[:, :, bass.ds(32 * g + DK * r, DK)], 1.0, None,
                                              ALU.mult)
                    e.then_inc(sem("at_values"), 1)
                    for w in range(2):
                        src, dst = (at_q, at_k)[w], (qst, kst)[w]
                        dve.wait_ge(sem("at_proj_copied%d" % w), 2 * ng)
                        dve.tensor_copy(hi[:, :], src).then_inc(sem("at_high%d" % w), 1)
                        dve.wait_ge(sem("at_high%d" % w), ng)
                        dve.tensor_scalar(sq[:, 1, :, :].rearrange("p h d -> p (h d)"), hi[:, :].bitcast(F32),
                                          stackc[:, 2 * w + 1:2 * w + 2], None, ALU.mult).then_inc(
                            sem("at_high_part%d" % w), 1)
                        dve.wait_ge(sem("at_high_part%d" % w), ng)
                        dve.scalar_tensor_tensor(dst[:, :], src, stackc[:, 2 * w:2 * w + 1],
                                                 sq[:, 1, :, :].rearrange("p h d -> p (h d)"), ALU.mult,
                                                 ALU.add).then_inc(sem("at_stacked%d" % w), 1)
                    dve.wait_ge(sem("at_stacked0"), ng)
                    dve.memset(spare[:, :], 0.0)
                    with dve.Fori(0, TPB) as t:
                        n = UNITS * b + TPB * g + t + 1
                        dve.tensor_copy(qtile[:, :], qst[:, bass.ts(t, P)].bitcast(F32)).then_inc(
                            sem("at_qtile"), 1)
                        for r in range(GQ):
                            dve.wait_ge(sem("at_scores"), 4 * (n - 1) + r + 1)
                            dve.tensor_reduce(amax[:, r:r + 1], psum[:, 2 * (r % 2):2 * (r % 2) + 2, :].rearrange(
                                "p a b -> p (a b)"), AX.X, ALU.max, negate=True).then_inc(
                                sem("at_maxima"), 1)
                            if r:
                                keep_pT_dve(dve, n, r - 1)
                        keep_pT_dve(dve, n, GQ - 1)
                        dve.wait_ge(sem("at_o_turned"), n)
                        o = bank[7][:, 0:P].rearrange("p (r c) -> p r c", c=32)
                        dve.reciprocal(orec[:, :], o[:, :, DK]).then_inc(sem("at_orec"), 1)
                        dve.wait_ge(sem("at_orec"), n)
                        dve.tensor_tensor(at_o[:, bass.ds(t, 1), bass.ds(32 * g, 32)].rearrange(
                            "p a (r d) -> p (a r) d", d=DK), o[:, :, 0:DK], bc(orec[:, :], DK), ALU.mult).then_inc(
                            sem("at_o"), 1)
                res = lin_k
                for h in range(2):
                    dve.wait_ge(sem("at_out%d" % h), b + 1)
                    dve.tensor_tensor(res[:, 4 * h:4 * h + 4, :], bank[2 + h][:, :].rearrange("p (a b) -> p a b", a=4),
                                      stage8[:, 4 * h:4 * h + 4, :], ALU.add).then_inc(sem("at_res"), 1)
                dve.wait_ge(sem("at_res"), 2 * (b + 1))
                dve.tensor_tensor(res, res, bias[:, 1, :].unsqueeze(1).broadcast_to([P, TPB, D]),
                                  ALU.add).then_inc(sem("at_biased"), 1)
                dve.wait_ge(sem("at_biased"), b + 1)
                for i in range(TPB):
                    e = dve.bn_stats(stt[:, i, :], res[:, i, :])
                e.then_inc(sem("at_stats"), 1)
                dve.wait_ge(sem("at_stats"), b + 1)
                dve.memset(spare[:, :], 0.0)
                for i in range(TPB):
                    e = dve.bn_aggr(mv8[:, i, :], stt[:, i, :])
                e.then_inc(sem("at_moments"), 1)
                dve.wait_ge(sem("at_rstd"), b + 1)
                for i in range(TPB):
                    dve.tensor_scalar(res[:, i, :], res[:, i, :], mv8[:, i, 0:1], rstd8[:, i:i + 1],
                                      ALU.subtract, ALU.mult).then_inc(sem("at_renormed"), 1)
                dve.wait_ge(sem("at_renormed"), TPB * (b + 1))
                dve.tensor_tensor(res, res, bias[:, 2, :].unsqueeze(1).broadcast_to([P, TPB, D]),
                                  ALU.mult).then_inc(sem("at_scaled"), 1)
                dve.wait_ge(sem("at_scaled"), b + 1)
                dve.tensor_tensor(res, res, bias[:, 3, :].unsqueeze(1).broadcast_to([P, TPB, D]),
                                  ALU.add).then_inc(sem("at_shifted"), 1)
                dve.wait_ge(sem("at_shifted"), b + 1)
                xs = X[:, bass.ds((TPB + 1) * b + 1, TPB), :]
                dve.tensor_tensor(xs, xs, res, ALU.add)

        def keep_pT_dve(dve, n, r):
            dve.wait_ge(sem("at_p_turnedb"), 4 * (n - 1) + r + 1)
            dve.tensor_copy(at_pT[1][:, :, r, :], bank[5][:, :].rearrange("p (a b) -> p a b", a=4)).then_inc(
                sem("at_pT_b"), 1)

        def attention2_pool(pool):
            with pool.Fori(0, BATCH) as b:
                pool.wait_ge(sem("at_moments"), b + 1)
                pool.tensor_tensor(rstd8[:, :], mv8[:, :, 1], eps[:, 0:TPB], ALU.add).then_inc(sem("at_var"), 1)
                pool.wait_ge(sem("at_var"), b + 1)
                pool.tensor_tensor(rstd8[:, :], rstd8[:, :], half[:, 0:TPB], ALU.pow).then_inc(sem("at_rstd"), 1)

        block = ctx.enter_context(nc.Block())

        @block.sync
        def _(sp):
            sync_program(sp)

        @block.tensor
        def _(pe):
            pe.wait_ge(sem("const_loaded"), LOADS)
            for i in range(16):
                mm = pe.transpose(bank[i // 4][:, P * (i % 4):P * (i % 4) + P], pTo[:, i, :], ident[:, :])
                mm.then_inc(sem("weights_turned"), 1)
            pe.transpose(bank[4][:, 0:NE], ystage[0:NE, :], ident[0:NE, 0:NE]).then_inc(sem("weights_turned"), 1)
            finish_phase(pe, 1)
            for i, (kind, c) in enumerate(STAGES):
                p0 = first_phase[i]
                finish_phase(pe, p0)
                if kind == "macaron":
                    with pe.Fori(0, DEPTH) as layer:
                        attention_pe(pe, c, layer)
                        finish_phase(pe, p0 + 1 + 2 * layer)
                        unit_pe(pe, c, layer)
                        finish_phase(pe, p0 + 2 + 2 * layer)
                    finish_phase(pe, p0 + 1 + 2 * DEPTH)
                    continue
                if kind == "linear":
                    linear_pe(pe)
                elif kind == "experts":
                    experts_pe(pe, c)
                else:
                    attention2_pe(pe)
                finish_phase(pe, p0 + 1)

        @block.scalar
        def _(act):
            for i in range(4):
                act.wait_ge(sem("weights_turned"), 4 * i + 4)
                act.activation(wT[:, 4 * i:4 * i + 4, :], bank[i][:, :].rearrange("p (a b) -> p a b", a=4), ACT.Copy)
            act.wait_ge(sem("weights_turned"), 17)
            act.activation(wrT[:, :], bank[4][:, 0:NE], ACT.Copy)
            finish_phase(act, 1)
            for i, (kind, c) in enumerate(STAGES):
                p0 = first_phase[i]
                finish_phase(act, p0)
                if kind == "macaron":
                    with act.Fori(0, DEPTH) as layer:
                        attention_act(act, c, layer)
                        finish_phase(act, p0 + 1 + 2 * layer)
                        unit_act(act, c, layer)
                        finish_phase(act, p0 + 2 + 2 * layer)
                    finish_phase(act, p0 + 1 + 2 * DEPTH)
                    continue
                if kind == "linear":
                    linear_act(act)
                elif kind == "experts":
                    experts_act(act, c)
                else:
                    attention2_act(act)
                finish_phase(act, p0 + 1)

        @block.vector
        def _(dve):
            vector_engine[0] = dve
            dve.memset(Y[:, :, :], 0.0)
            dve.memset(Z[:, :, :], 0.0)
            dve.memset(prob[:, :, :], 0.0)
            for i in range(2):
                dve.memset(kT[i][:, :, :], 0.0)
                dve.memset(V[i][:, :], 0.0)
            dve.memset(gT[:, 2, :], 1.0)
            dve.memset(half[:, :], -0.5)
            dve.memset(eps[:, :], LN_EPS)
            dve.memset(waste[:, :], 0.0)
            dve.memset(ones[:, :], 1.0)
            dve.wait_ge(sem("const_loaded"), LOADS)
            dve.tensor_copy(identb[:, :], ident[:, :])
            dve.tensor_copy(selb[:, :, :], sel[:, :, :])
            for t in range(TILES):
                m = 0 if t % TPB == 0 else 1
                dve.tensor_copy(mask[:, t, :], masks[:, m * KEYS:(m + 1) * KEYS])
            finish_phase(dve, 1)
            for i, (kind, c) in enumerate(STAGES):
                p0 = first_phase[i]
                stats_dve(dve, i + 1)
                if kind == "macaron":
                    norm_dve(dve, i + 1)
                    finish_phase(dve, p0)
                    with dve.Fori(0, DEPTH) as layer:
                        attention_dve(dve, c, layer)
                        finish_phase(dve, p0 + 1 + 2 * layer)
                        unit_dve(dve, c, layer)
                        finish_phase(dve, p0 + 2 + 2 * layer)
                    for b in range(BATCH):
                        dve.scalar_tensor_tensor(rows(X)[:, b], rows(Y)[:, b], 0.5, rows(X)[:, b], ALU.mult, ALU.add)
                    finish_phase(dve, p0 + 1 + 2 * DEPTH)
                    continue
                finish_phase(dve, p0)
                if kind == "linear":
                    linear_dve(dve)
                elif kind == "experts":
                    experts_dve(dve, c)
                else:
                    attention2_dve(dve)
                finish_phase(dve, p0 + 1)

        @block.gpsimd
        def _(pool):
            finish_phase(pool, 1)
            for i, (kind, c) in enumerate(STAGES):
                p0 = first_phase[i]
                stats_pool(pool, i + 1)
                finish_phase(pool, p0)
                if kind == "macaron":
                    with pool.Fori(0, DEPTH) as layer:
                        attention_pool(pool, c, layer)
                        finish_phase(pool, p0 + 1 + 2 * layer)
                        pool.tensor_tensor(waste[:, 0:1], waste[:, 1:2], eps[:, 0:1], ALU.mult)
                        finish_phase(pool, p0 + 2 + 2 * layer)
                    finish_phase(pool, p0 + 1 + 2 * DEPTH)
                    continue
                if kind == "attention":
                    attention2_pool(pool)
                finish_phase(pool, p0 + 1)


_INS = ['L0_attn_x', 'L0_attn_W_qkv', 'L0_attn_W_out', 'L0_attn_b_out', 'L0_ffn_Wqkv', 'L0_ffn_q_scale',
        'L0_ffn_k_scale', 'L0_ffn_Wo', 'L0_ffn_ln_g', 'L0_ffn_ln_b', 'L0_ffn_W1', 'L0_ffn_b1', 'L0_ffn_W2',
        'L0_ffn_b2', 'L1_attn_w_q', 'L1_attn_w_k', 'L1_attn_w_v', 'L1_attn_w_o', 'L1_attn_b_o',
        'L1_attn_ln_g', 'L1_attn_ln_b', 'L1_ffn_w_router', 'L1_ffn_w_fc', 'L1_ffn_w_proj']


def shape_constants():
    import numpy as np
    f = np.float32
    tri = np.zeros((P, 400 + 4 * TPB * DH), f)
    tri[:, 0:128] = np.eye(P)
    tri[:, 128:256] = np.eye(P, k=1)
    tri[P - 1, 256] = 1.0
    tri[:, 384:400] = (np.arange(TILES) % TPB != 0)[None, :]
    pair = np.arange(0, DH, 2, dtype=f)
    inv_freq = (f(1.0) / (f(10000.0) ** (pair / f(DH)))).astype(f)
    t = np.arange(SEQ, dtype=f)
    freqs = (t[:, None] * inv_freq[None, :]).astype(f)
    base = ((pair + f(0.4 * DH)) / f(1.4 * DH)).astype(f)
    power = (t - f(SEQ // 2)) / f(WIN // 2)
    scale = (base[None, :] ** power[:, None]).astype(f)
    cos, sin = np.cos(freqs).astype(f), np.sin(freqs).astype(f)
    inv = (f(1.0) / scale).astype(f)
    tabs = [np.concatenate([a, b], -1) for a, b in (
        (f(8.0) * cos * scale, f(8.0) * cos * scale), (-f(8.0) * sin * scale, f(8.0) * sin * scale),
        (cos * inv, cos * inv), (-sin * inv, sin * inv))]
    tri[:, 400:] = np.stack([a.reshape(TPB, P, DH).transpose(1, 0, 2) for a in tabs], 1).reshape(P, -1)
    i = np.arange(P)[:, None]
    j = np.arange(KEYS)[None, :] - WIN
    seen = (j <= i) & (j >= i - WIN)
    masks = np.concatenate([np.where(seen & (j >= 0), 0.0, NEG), np.where(seen, 0.0, NEG)], 1)
    extra = np.zeros((P, NE + 4 + 4 * P), f)
    extra[:, 0:NE] = NE - np.arange(NE)[None, :]
    copy = np.arange(P) // DK % 4
    for w, low in enumerate((copy >= 2, copy % 2 == 1)):
        extra[:, NE + 2 * w] = low
        extra[:, NE + 2 * w + 1] = np.where(low, -1.0, 1.0)
    for m in range(4):
        for e in range(2):
            extra[2 * m + e, NE + 4 + P * m + EH * e:NE + 4 + P * m + EH * e + EH] = 1.0
    return tri, np.concatenate([masks, extra], 1).astype(f)


def kernel(**inputs):
    import numpy as _np
    import concourse.bacc as _bacc
    from concourse import mybir as _mybir
    from concourse.bass_utils import run_bass_kernel_spmd as _run

    nc = _bacc.Bacc("TRN2", target_bir_lowering=False, num_devices=1)
    arrays, args = {}, {}
    consts, masks = shape_constants()
    named = {name: _np.ascontiguousarray(inputs[name]) for name in _INS}
    named["shape_consts"] = consts
    named["shape_masks"] = masks
    for name, a in named.items():
        arrays[f"in_{name}_dram"] = a
        args[name] = nc.dram_tensor(f"in_{name}_dram", a.shape, _mybir.dt.from_np(a.dtype), kind="ExternalInput").ap()
    o = nc.dram_tensor("out_0_dram", (BATCH, SEQ, D), _mybir.dt.float32, kind="ExternalOutput").ap()
    W = {k.replace("L0_ffn_", ""): v for k, v in args.items() if k.startswith("L0_ffn_")}
    W.update({k: v for k, v in args.items() if not k.startswith("L0_ffn_")})
    build(nc, args["L0_attn_x"], W, args["shape_consts"], args["shape_masks"], o)
    r = _run(nc, [arrays], core_ids=[0])
    return r.results[0]["out_0_dram"]
```

```python
from contextlib import ExitStack

import concourse.bass as bass
from concourse import mybir

ALU = mybir.AluOpType
ACT = mybir.ActivationFunctionType
AX = mybir.AxisListType
F32 = mybir.dt.float32
F32R = mybir.dt.float32r
BF16 = mybir.dt.bfloat16

P = 128
D = 128
HALF = D // 2
BATCH = 2
SEQ = 1024
TPB = SEQ // P
TILES = BATCH * TPB
DEPTH = 6
HEADS = 16
DH = 64
RH = DH // 2
WIN = 32
INNER = HEADS * DH
KEYS = WIN + P
PADK = P - WIN
DI = int(D * 4 * 2 / 3)
FC = [(0, P), (P, P), (2 * P, DI - 2 * P)]
LAST = DI - 2 * P
SLOTS = 20
NEG = -1e35
LN_EPS = 1e-5
LIN_EPS = 1e-6
PAIRS = HEADS // 2
ORDER = [h for p0, p1 in ((0, 3), (3, 6), (6, 8)) for r in range(2) for h in range(2 * p0 + r, 2 * p1, 2)]
PLACE = [ORDER.index(h) for h in range(HEADS)]
SG = [(0, 3), (3, 6), (6, 9), (9, 12), (12, 14), (14, 16)]
NG = [(0, 6), (6, 12), (12, 16)]
NE = 8
EH = 64
H2 = 16
DK = D // H2
GQ = 4
NKB = SEQ // P


def slot(t):
    return t + 1 + (t >> 3)


STAGES = [("macaron", 0), ("linear", 0), ("macaron", 1), ("experts", 0), ("attention", 0), ("experts", 1)]


PARTS = dict(scores=6, maxima=6, exp_done=6, projected=4, proj_copied=4, v_projected=2, v_ready=2, p_turned=5,
             pT_ready=5, qk_turned=4, sine_part=4, normalised=3, inverted=3, cosine_part=2, turned_sum=2,
             squared=2, summed=2, norms_squared=2, rnorm=2, qk_rotated=2, qT_ready=2, kT_ready=2, attended=2,
             aT_ready=2)


class Tiles:

    def __init__(self, done_before):
        self.done_before = done_before
        self.r = 0

    def tile(self, k):
        return self.r + k

    def part(self, k, name, i=0):
        return PARTS.get(name, 1) * (self.done_before + self.r + k) + (i + 1)


LOOPED = 10


def run_steps(eng, tiles, step, rings=()):
    for k in range(-2, 4):
        step(k)
    with eng.Fori(0, LOOPED - 1, 2) as r:
        tiles.r = r
        step(4)
        step(5)
    tiles.r = 0
    for ring in rings:
        for bank in ring:
            ring[bank] = [(s, k + LOOPED - 2, i) for s, k, i in ring[bank]]
    for k in range(4 + LOOPED, TILES + 3):
        step(k)


def build(nc, x_in, W, const, maskc, out):
    with ExitStack() as ctx:
        def sb(name, shape, dt=F32):
            return ctx.enter_context(nc.sbuf_tensor(name, shape, dt))

        sems = {}

        def sem(name):
            if name not in sems:
                sems[name] = ctx.enter_context(nc.semaphore(name))
            return sems[name]

        psum = ctx.enter_context(nc.psum_tensor("psum", [P, 8, 512], F32))
        bank = [psum[:, i, :] for i in range(8)]

        X = sb("X", [P, SLOTS, D])
        Y = sb("Y", [P, SLOTS, D])
        Z = sb("Z", [P, SLOTS, D])
        ident = sb("ident", [P, P])
        shift1 = sb("shift1", [P, P])
        lastrow = sb("lastrow", [P, P])
        keepk = sb("keepk", [P, TILES])
        rope = sb("rope", [P, 4, TPB, DH])
        identb = sb("identb", [P, P], BF16)
        mask = sb("mask", [P, TILES, KEYS], BF16)
        half = sb("half", [P, 32])
        eps = sb("eps", [P, TILES])
        carrier = sb("carrier", [P, 2])
        spare = sb("spare", [P, 1])
        wqkv = sb("wqkv", [P, 3 * INNER])
        wo = sb("wo", [P, PAIRS, D])
        w1 = sb("w1", [P, 2 * DI])
        w2 = sb("w2", [P, 3, D])
        lng = sb("lng", [P, 1])
        lnb = sb("lnb", [P, 1])
        b1 = sb("b1", [P, 6])
        qks = sb("qks", [P, 2, DH])
        ropes = sb("ropes", [P, 4, TPB, DH])
        ystage = sb("ystage", [P, D])
        xT = [sb(f"xT{i}", [P, P + 1]) for i in range(2)]
        raw = sb("raw", [P, 2, HEADS, DH])
        sq = sb("sq", [P, 2, HEADS, DH])
        rot = sb("rot", [P, 2, HEADS, DH])
        qkr = sb("qkr", [P, 2, HEADS, DH])
        ss = sb("ss", [P, 32])
        rn = sb("rn", [P, 32])
        qT = sb("qT", [P, PAIRS, P])
        kT = [sb(f"kT{i}", [P, PAIRS, KEYS]) for i in range(2)]
        V = [sb(f"V{i}", [P, INNER]) for i in range(2)]
        prob = sb("prob", [P, HEADS, 2 * P])
        nmax = sb("nmax", [P, HEADS])
        den = sb("den", [P, HEADS])
        rden = sb("rden", [P, HEADS])
        pTo = sb("pTo", [P, HEADS, P])
        pTp = sb("pTp", [P, HEADS, WIN])
        aT = sb("aT", [P, PAIRS, P])
        zstage = sb("zstage", [P, D])
        zn = sb("zn", [P, D])
        st6 = sb("st6", [P, 6])
        mv = sb("mv", [P, 2])
        rstd1 = sb("rstd1", [P, 2])
        xnT = sb("xnT", [P, TILES * P])
        gel = sb("gel", [P, 3, 512])
        gT = sb("gT", [P, 3, 512])
        masks = pTp[:, :, :].rearrange("p a b -> p (a b)")[:, 0:2 * KEYS]
        LOADS = 16 * 24
        mv8 = sb("mv8", [P, TPB, 2])
        rstd8 = sb("rstd8", [P, TPB])
        stt = sb("stt", [P, TILES, 6])
        mva = sb("mva", [P, TILES + 2, 2])
        rstda = sb("rstda", [P, TILES])
        wT = sb("wT", [P, 16, P])
        wrT = sb("wrT", [P, NE])
        bias = sb("bias", [P, 4, D])
        kvT = sb("kvT", [P, D])
        mixk = sb("mixk", [P, D + 1])
        ones = sb("ones", [P, 1])
        zden = sb("zden", [P, 4, 2])
        sel = sb("sel", [NE, 4, P])
        selb = sb("selb", [NE, 4, P], BF16)
        erank = sb("erank", [P, NE])
        lmax = sb("lmax", [P, 4])
        cand = sb("cand", [P, 4, NE])
        onehot = sb("onehot", [P, 4, NE])
        onehotT = sb("onehotT", [NE, 4, P], BF16)
        stackc = sb("stackc", [P, 4])
        wst = sb("wst", [P, 2, P])
        qst = sb("qst", [P, SEQ], F32R)
        kst = sb("kst", [P, SEQ], F32R)
        hi = V[0][:, :].bitcast(F32R)
        qtile = [sb(f"qtile{i}", [P, P], F32R) for i in range(2)]
        vg = V[1][:, :].rearrange("p (k r c) -> p k r c", k=NKB, r=GQ)
        oT = sb("oT", [P, P])
        orec = sb("orec", [P, GQ])
        amax = sb("amax", [P, GQ])

        phase = sem("phase_done")

        def finish_phase(eng, n):
            eng.drain().then_inc(phase, 1)
            eng.wait_ge(phase, 4 * n)

        def finish_phase_dve(dve, n):
            finish_phase(dve, n)
            dve.memset(spare[:, :], 0.0)

        first_phase, n = [], 2
        for kind, _ in STAGES:
            first_phase.append(n)
            n += 2 + 2 * DEPTH if kind == "macaron" else 2
        END = n - 1
        macaron_at = [first_phase[i] for i, (kind, _) in enumerate(STAGES) if kind == "macaron"]

        def bc(ap, n):
            return ap.unsqueeze(2).broadcast_to([ap.shape[0], ap.shape[1], n])

        def rows(buf):
            return buf[:, 0:2 * (TPB + 1), :].rearrange("p (b s) f -> p b s f", b=BATCH)[:, :, 1:, :]

        def sync_program(sp):
            ld = sem("const_loaded")
            sp.dma_start(ident[:, :], const[:, 0:128]).then_inc(ld, 16)
            sp.dma_start(shift1[:, :], const[:, 128:256]).then_inc(ld, 16)
            sp.dma_start(lastrow[:, :], const[:, 256:384]).then_inc(ld, 16)
            sp.dma_start(keepk[:, :], const[:, 384:400]).then_inc(ld, 16)
            sp.dma_start(rope[:, :, :, :].rearrange("p a t d -> p (a t d)"),
                         const[:, 400:400 + 4 * TPB * DH]).then_inc(ld, 16)
            xv = x_in.rearrange("b (s p) f -> p (b s) f", p=P)
            sp.dma_start(X[:, 1:TPB + 1, :], xv[:, 0:TPB, :]).then_inc(ld, 16)
            sp.dma_start(X[:, TPB + 2:2 * TPB + 2, :], xv[:, TPB:, :]).then_inc(ld, 16)
            sp.dma_start(masks, maskc[:, 0:2 * KEYS]).then_inc(ld, 16)
            for i, (name, m) in enumerate((("L0_attn_W_qkv", 3), ("L0_attn_W_out", 1), ("L1_attn_w_q", 1),
                                           ("L1_attn_w_k", 1), ("L1_attn_w_v", 1), ("L1_attn_w_o", 1))):
                at = [0, 3, 4, 5, 6, 7][i]
                sp.dma_start(pTo[:, at:at + m, :], W[name].rearrange("(m p) d -> p m d", p=P)).then_inc(ld, 16)
            sp.dma_start(pTo[:, 8:12, :], W["L1_ffn_w_fc"].rearrange("(m e) h d -> (e h) m d", m=4)).then_inc(ld, 16)
            sp.dma_start(pTo[:, 12:16, :].rearrange("p m (e h) -> p (m e) h", e=2),
                         W["L1_ffn_w_proj"].rearrange("e d h -> d e h")).then_inc(ld, 16)
            sp.dma_start(ystage[0:NE, :], W["L1_ffn_w_router"]).then_inc(ld, 16)
            for i, name in enumerate(("L0_attn_b_out", "L1_attn_b_o", "L1_attn_ln_g", "L1_attn_ln_b")):
                sp.dma_start(bias[:, i, :], W[name].partition_broadcast(P)).then_inc(ld, 16)
            sp.dma_start(erank[:, :], maskc[:, 2 * KEYS:2 * KEYS + NE]).then_inc(ld, 16)
            sp.dma_start(stackc[:, :], maskc[:, 2 * KEYS + NE:2 * KEYS + NE + 4]).then_inc(ld, 16)
            sp.dma_start(sel[:, :, :].rearrange("p a b -> p (a b)"),
                         maskc[0:NE, 2 * KEYS + NE + 4:2 * KEYS + NE + 4 + 4 * P]).then_inc(ld, 16)
            for c in range(len(macaron_at)):
                with sp.Fori(0, DEPTH) as layer:
                    sp.wait_ge(phase, 4 * (macaron_at[c] - 1) + 8 * layer)
                    load_attention_weights(sp, c, layer)
                    sp.wait_ge(phase, 4 * macaron_at[c] + 8 * layer)
                    load_unit_weights(sp, c, layer)
            sp.wait_ge(phase, 4 * END)
            ov = out.rearrange("b (s p) f -> p (b s) f", p=P)
            sp.dma_start(ov[:, 0:TPB, :], X[:, 1:TPB + 1, :]).then_inc(sem("stored"), 16)
            sp.dma_start(ov[:, TPB:, :], X[:, TPB + 2:2 * TPB + 2, :]).then_inc(sem("stored"), 16)
            sp.wait_ge(sem("stored"), 32)

        AW = 4

        def load_attention_weights(sp, c, layer):
            s = sem("attn_weights")
            sp.dma_start(wqkv[:, :], W["Wqkv"][layer, :, :]).then_inc(s, 16)
            sp.dma_start(wo[:, :, :], W["Wo"][layer, :, :].rearrange("(c p) f -> p c f", p=P)).then_inc(s, 16)
            sp.dma_start(qks[:, 0, :], W["q_scale"][layer, :].partition_broadcast(P)).then_inc(s, 16)
            sp.dma_start(qks[:, 1, :], W["k_scale"][layer, :].partition_broadcast(P)).then_inc(s, 16)

        UW = 12

        def load_unit_weights(sp, c, layer):
            s = sem("unit_weights")
            sp.dma_start(w1[:, :], W["W1"][layer, :, :]).then_inc(s, 16)
            sp.dma_start(w2[:, 0:2, :], W["W2"][layer, 0:2 * P, :].rearrange("(c p) f -> p c f", p=P)).then_inc(s, 16)
            sp.dma_start(w2[0:LAST, 2, :], W["W2"][layer, 2 * P:DI, :]).then_inc(s, 16)
            sp.dma_start(w2[LAST:LAST + 1, 2, :], W["b2"][bass.ds(layer, 1), :]).then_inc(s, 16)
            sp.dma_start(lng[:, :], W["ln_g"][layer, :].unsqueeze(1)).then_inc(s, 16)
            sp.dma_start(lnb[:, :], W["ln_b"][layer, :].unsqueeze(1)).then_inc(s, 16)
            for h in range(2):
                for i, (c0, m) in enumerate(FC):
                    sp.dma_start(b1[0:m, 3 * h + i:3 * h + i + 1],
                                 W["b1"][layer, h * DI + c0:h * DI + c0 + m].unsqueeze(1)).then_inc(s, 16)

        SHIFT_BANK, UNIT_BANK, QT_BANK, KT_BANK = 0, 1, (2, 0), (1, 2)
        PT_BANK, OUT_BANK, X_BANK, WO_BANK = (0, 1, 2, 0, 1), (2, 0), 1, 2

        def works_on(k):
            return [0 <= t < TILES for t in (k + 2, k + 1, k, k - 1, k - 2, k - 3)]

        def attention_pe(pe, c, layer):
            tl = Tiles(c * DEPTH * TILES + layer * TILES)
            part = tl.part
            small, score, proj = {}, {}, {}

            def refill(ring, b, emptied_by):
                for s, t, i in ring.get(b, []):
                    pe.wait_ge(sem(s), part(t, s, i))
                ring[b] = emptied_by

            pe.wait_ge(sem("attn_weights"), 16 * AW * (c * DEPTH + 1) + 16 * AW * layer)

            def score_groups(k, groups):
                for g in groups:
                    h0, h1 = SG[g]
                    b = 3 + g % 3
                    refill(score, b, [("exp_done", k, g)])
                    m = h1 - h0
                    pe.matmul(bank[b][:, 0:m * KEYS], identb[:, :],
                              mask[:, tl.tile(k), :].unsqueeze(1).broadcast_to([P, m, KEYS]),
                              start=True, stop=False, skip_group_check=True)
                    for i in range(m):
                        h = ORDER[h0 + i]
                        q0 = DH * (h % 2)
                        mm = pe.matmul(bank[b][:, i * KEYS:(i + 1) * KEYS], qT[q0:q0 + DH, h // 2, :],
                                       kT[k % 2][q0:q0 + DH, h // 2, :],
                                       start=False, stop=True, skip_group_check=True)
                    mm.then_inc(sem("scores"), 1)

            def project_qk(u, q):
                refill(proj, 6 + q % 2, [("proj_copied", u, q)])
                pe.matmul(bank[6 + q % 2][:, :], xT[u % 2][:, 0:P], wqkv[:, 512 * q:512 * q + 512],
                          start=True, stop=True).then_inc(sem("projected"), 1)

            def turn_qk(t, w):
                pe.wait_ge(sem("qk_rotated"), part(t, "qk_rotated", w))
                for i in range(2):
                    b = (QT_BANK, KT_BANK)[w][i]
                    refill(small, b, [(("qT_ready", "kT_ready")[w], t, i)])
                    for j in range(4):
                        p = 4 * i + j
                        src = qkr[:, w, 2 * p:2 * p + 2, :].rearrange("p a d -> p (a d)")
                        mm = pe.transpose(bank[b][:, P * j:P * j + P], src, ident[:, :])
                    mm.then_inc(sem("qk_turned"), 1)

            def turn_p(t, g):
                b = PT_BANK[g + (g > 0)]
                for i in range(4):
                    mm = pe.transpose(bank[b][:, P * i:P * i + P], prob[:, 4 * g + i, P:2 * P], ident[:, :])
                mm.then_inc(sem("p_turned"), 1)

            def step(k):
                has_x, has_u, has_t, has_o, has_v, has_z = works_on(k)
                x, u, o, v, z = k + 2, k + 1, k - 1, k - 2, k - 3
                if has_v:
                    refill(small, SHIFT_BANK, [("unit_staged", v, 0)])
                    b = bank[SHIFT_BANK]
                    sv = slot(tl.tile(v))
                    pe.wait_ge(sem("attn_added"), part(v, "attn_added"))
                    pe.matmul(b[:, HALF:D], shift1[:, :], Z[:, sv, HALF:D], start=True, stop=False)
                    pe.matmul(b[:, HALF:D], lastrow[:, :], Z[:, sv - 1, HALF:D],
                              start=False, stop=True).then_inc(sem("unit_shifted"), 1)
                if has_u:
                    pe.wait_ge(sem("xT_ready"), part(u, "xT_ready"))
                    project_qk(u, 0)
                    project_qk(u, 1)
                if has_z:
                    refill(small, UNIT_BANK, [("xnT_ready", z, 0)])
                    pe.wait_ge(sem("unit_normed"), part(z, "unit_normed"))
                    pe.transpose(bank[UNIT_BANK][:, 0:P], zn[:, :], ident[:, :]).then_inc(sem("unit_turned"), 1)
                if has_t:
                    turn_qk(k, 0)
                if has_u:
                    project_qk(u, 2)
                if has_t:
                    turn_qk(k, 1)
                if has_u:
                    project_qk(u, 3)
                if has_o:
                    refill(small, PT_BANK[1], [("pT_ready", o, 1)])
                    refill(small, PT_BANK[0], [("pT_ready", o, 0)])
                    pe.wait_ge(sem("normalised"), part(o, "normalised", 2))
                    turn_p(o, 0)
                    for h in range(HEADS):
                        mm = pe.transpose(bank[PT_BANK[1]][:, WIN * h:WIN * h + WIN], prob[0:WIN, h, 0:P],
                                          ident[0:WIN, 0:WIN])
                    mm.then_inc(sem("p_turned"), 1)
                    refill(small, PT_BANK[2], [("pT_ready", o, 2)])
                    turn_p(o, 1)
                    for g in (2, 3):
                        refill(small, PT_BANK[g + 1], [("pT_ready", o, g + 1)])
                        turn_p(o, g)
                if has_t:
                    for q in range(2):
                        refill(proj, 6 + q, [("v_ready", k, q)])
                        pe.matmul(bank[6 + q][:, :], xT[k % 2][:, 0:P],
                                  wqkv[:, 2 * INNER + 512 * q:2 * INNER + 512 * q + 512],
                                  start=True, stop=True).then_inc(sem("v_projected"), 1)
                if has_o:
                    pe.wait_ge(sem("v_ready"), part(o, "v_ready", 1))
                    pe.wait_ge(sem("pT_ready"), part(o, "pT_ready", 4))
                    for e in range(2):
                        b = OUT_BANK[e]
                        refill(small, b, [("aT_ready", o, e)])
                        for p in range(4 * e, 4 * e + 4):
                            for h in (2 * p, 2 * p + 1):
                                q0 = DH * (h % 2)
                                dst = bank[b][q0:q0 + DH, P * (p % 4):P * (p % 4) + P]
                                pe.matmul(dst, V[o % 2][:, DH * h:DH * h + DH], pTo[:, PLACE[h], :],
                                          start=True, stop=False, skip_group_check=True)
                                mm = pe.matmul(dst[:, 0:WIN], V[1 - o % 2][:, DH * h:DH * h + DH],
                                               pTp[:, PLACE[h], :], start=False, stop=True,
                                               skip_group_check=True)
                        mm.then_inc(sem("attended"), 1)
                if has_t:
                    pe.wait_ge(sem("qT_ready"), part(k, "qT_ready", 1))
                    pe.wait_ge(sem("kT_ready"), part(k, "kT_ready", 1))
                    pe.wait_ge(sem("k_carried"), part(k, "k_carried"))
                    score_groups(k, (0, 1, 2))
                if has_x:
                    refill(small, X_BANK, [("xT_ready", x, 0)])
                    pe.wait_ge(sem("input_staged"), part(x, "input_staged"))
                    pe.transpose(bank[X_BANK][:, 0:P], ystage[:, :], ident[:, :]).then_inc(sem("x_turned"), 1)
                if has_o:
                    refill(small, WO_BANK, [("attn_added", o, 0)])
                    pe.wait_ge(sem("aT_ready"), part(o, "aT_ready", 1))
                    for p in range(PAIRS):
                        mm = pe.matmul(bank[WO_BANK][:, 0:D], aT[:, p, :], wo[:, p, :], start=(p == 0),
                                       stop=(p == PAIRS - 1))
                    mm.then_inc(sem("attn_out"), 1)
                if has_t:
                    score_groups(k, (3, 4, 5))

            run_steps(pe, tl, step, (small, score, proj))

        def four(b):
            return bank[b][:, :].rearrange("p (a b) -> p a b", a=4)

        def attention_act(act, c, layer):
            tl = Tiles(c * DEPTH * TILES + layer * TILES)
            part = tl.part
            act.wait_ge(sem("unit_weights"), 16 * UW * (c * DEPTH + 1) + 16 * UW * layer)

            def step(k):
                has_x, has_u, has_t, has_o, has_v, has_z = works_on(k)
                u, o, z = k + 1, k - 1, k - 3
                def keep_qk(q):
                    if has_t and q % 2 == 0:
                        act.wait_ge(sem("cosine_part"), part(k, "cosine_part", q // 2))
                        act.wait_ge(sem("sine_part"), part(k, "sine_part", q + 1))
                    act.wait_ge(sem("projected"), part(u, "projected", q))
                    act.activation(raw[:, q // 2, 8 * (q % 2):8 * (q % 2) + 8, :],
                                   bank[6 + q % 2][:, :].rearrange("p (a b) -> p a b", a=8),
                                   ACT.Copy).then_inc(sem("proj_copied"), 1)

                def square(w):
                    act.wait_ge(sem("proj_copied"), part(u, "proj_copied", 2 * w + 1))
                    if has_t:
                        act.wait_ge(sem("turned_sum"), part(k, "turned_sum", w))
                    act.activation(sq[:, w, :, :], raw[:, w, :, :], ACT.Square).then_inc(sem("squared"), 1)

                def keep_p(*fills):
                    for f in fills:
                        act.wait_ge(sem("p_turned"), part(o, "p_turned", f))
                        if f == 1:
                            e = act.activation(pTp[:, :, :], bank[PT_BANK[1]][:, :].rearrange(
                                "p (a b) -> p a b", b=WIN), ACT.Copy)
                        else:
                            g = max(f - 1, 0)
                            e = act.activation(pTo[:, 4 * g:4 * g + 4, :], four(PT_BANK[f]), ACT.Copy)
                        e.then_inc(sem("pT_ready"), 1)

                if has_u:
                    keep_qk(0)
                    keep_qk(1)
                if has_z:
                    act.wait_ge(sem("unit_turned"), part(z, "unit_turned"))
                    act.activation(xnT[:, bass.ts(tl.tile(z), P)], bank[UNIT_BANK][:, 0:P], ACT.Identity,
                                   bias=lnb[:, 0:1], scale=lng[:, 0:1]).then_inc(sem("xnT_ready"), 1)
                if has_t:
                    for i in range(2):
                        act.wait_ge(sem("qk_turned"), part(k, "qk_turned", i))
                        act.activation(qT[:, 4 * i:4 * i + 4, :], four(QT_BANK[i]),
                                       ACT.Copy).then_inc(sem("qT_ready"), 1)
                if has_u:
                    square(0)
                    keep_qk(2)
                    keep_qk(3)
                if has_o:
                    keep_p(0, 1, 2, 3, 4)
                if has_u:
                    square(1)
                if has_t:
                    for q in range(2):
                        if has_o:
                            act.wait_ge(sem("attended"), part(o, "attended", 1))
                        act.wait_ge(sem("v_projected"), part(k, "v_projected", q))
                        act.activation(V[k % 2][:, 512 * q:512 * q + 512], bank[6 + q][:, :],
                                       ACT.Copy).then_inc(sem("v_ready"), 1)
                    for g, (h0, h1) in enumerate(SG):
                        act.wait_ge(sem("maxima"), part(k, "maxima", g))
                        for i, h in enumerate(range(h0, h1)):
                            e = act.activation(prob[:, h, PADK:2 * P],
                                               bank[3 + g % 3][:, i * KEYS:(i + 1) * KEYS], ACT.Exp,
                                               bias=nmax[:, h:h + 1], accum_out=den[:, h:h + 1])
                        e.then_inc(sem("exp_done"), 1)

            run_steps(act, tl, step)

        def attention_dve(dve, c, layer):
            tl = Tiles(c * DEPTH * TILES + layer * TILES)
            part = tl.part
            dve.wait_ge(sem("attn_weights"), 16 * AW * (c * DEPTH + 1) + 16 * AW * layer)
            def scale_ropes():
                for w in range(2):
                    for tr in range(2):
                        for i in range(2):
                            o = ropes[:, 2 * w + tr, :, RH * i:RH * i + RH]
                            s = qks[:, w, RH * (i ^ tr):RH * (i ^ tr) + RH].unsqueeze(1).broadcast_to([P, TPB, RH])
                            e = dve.tensor_tensor(o, rope[:, 2 * w + tr, :, RH * i:RH * i + RH], s, ALU.mult)
                            e.then_inc(sem("ropes_scaled"), 1)
                dve.wait_ge(sem("ropes_scaled"), 8 * (c * DEPTH + 1) + 8 * layer)

            def step(k):
                has_x, has_u, has_t, has_o, has_v, has_z = works_on(k)
                x, u, o, v, z = k + 2, k + 1, k - 1, k - 2, k - 3

                def finish_rotation(w):
                    dve.wait_ge(sem("rnorm"), part(k, "rnorm", w))
                    dve.wait_ge(sem("turned_sum"), part(k, "turned_sum", w))
                    dve.tensor_tensor(qkr[:, w, :, :], rot[:, w, :, :], bc(rn[:, 16 * w:16 * w + 16], DH),
                                      ALU.mult).then_inc(sem("qk_rotated"), 1)

                def invert(t, j):
                    h0, h1 = NG[j]
                    dve.wait_ge(sem("exp_done"), part(t, "exp_done", 2 * j + 1))
                    dve.reciprocal(rden[:, h0:h1], den[:, h0:h1]).then_inc(sem("inverted"), 1)

                def maximum(g):
                    h0, h1 = SG[g]
                    dve.wait_ge(sem("scores"), part(k, "scores", g))
                    dve.tensor_reduce(nmax[:, h0:h1],
                                      bank[3 + g % 3][:, 0:(h1 - h0) * KEYS].rearrange("p (a b) -> p a b", b=KEYS),
                                      AX.X, ALU.max, negate=True).then_inc(sem("maxima"), 1)

                def length(w):
                    dve.wait_ge(sem("squared"), part(u, "squared", w))
                    dve.tensor_reduce(ss[:, 16 * w:16 * w + 16], sq[:, w, :, :], AX.X, ALU.add).then_inc(
                        sem("summed"), 1)
                    dve.wait_ge(sem("summed"), part(u, "summed", w))
                    dve.tensor_scalar(ss[:, 16 * w:16 * w + 16], ss[:, 16 * w:16 * w + 16], 1e-24, None,
                                      ALU.max).then_inc(sem("norms_squared"), 1)
                    ti = tl.tile(u) & 7
                    for i in range(2):
                        dve.tensor_tensor(sq[:, w, :, RH * i:RH * i + RH],
                                          raw[:, w, :, RH * (1 - i):RH * (1 - i) + RH],
                                          ropes[:, 2 * w + 1, bass.ds(ti, 1), RH * i:RH * i + RH].broadcast_to(
                                              [P, HEADS, RH]), ALU.mult).then_inc(sem("sine_part"), 1)

                def add_sines(w):
                    dve.wait_ge(sem("cosine_part"), part(u, "cosine_part", w))
                    dve.wait_ge(sem("sine_part"), part(u, "sine_part", 2 * w + 1))
                    dve.tensor_tensor(rot[:, w, :, :], rot[:, w, :, :], sq[:, w, :, :], ALU.add).then_inc(
                        sem("turned_sum"), 1)

                def keep_out(e):
                    dve.wait_ge(sem("attended"), part(o, "attended", e))
                    dve.tensor_copy(aT[:, 4 * e:4 * e + 4, :], four(OUT_BANK[e])).then_inc(sem("aT_ready"), 1)

                if has_z:
                    if k >= 4:
                        dve.wait_ge(sem("unit_turned"), part(z - 1, "unit_turned"))
                    dve.wait_ge(sem("unit_rstd"), part(z, "unit_rstd"))
                    dve.tensor_scalar(zn[:, :], zstage[:, :], mv[:, 0:1], rstd1[:, 1:2], ALU.subtract,
                                      ALU.mult).then_inc(sem("unit_normed"), 1)
                if has_t:
                    finish_rotation(0)
                if has_o:
                    invert(o, 1)
                    invert(o, 2)
                if has_v:
                    if has_z:
                        dve.wait_ge(sem("unit_normed"), part(z, "unit_normed"))
                    dve.wait_ge(sem("unit_shifted"), part(v, "unit_shifted"))
                    dve.tensor_copy(zstage[:, HALF:D], bank[SHIFT_BANK][:, HALF:D])
                    dve.tensor_copy(zstage[:, 0:HALF], Z[:, slot(tl.tile(v)), 0:HALF]).then_inc(
                        sem("unit_staged"), 1)
                if has_t:
                    finish_rotation(1)
                if has_t:
                    dve.tensor_scalar(kT[k % 2][:, :, 0:WIN], kT[1 - k % 2][:, :, P:KEYS],
                                      keepk[:, bass.ds(tl.tile(k), 1)], None, ALU.mult).then_inc(
                        sem("k_carried"), 1)
                if has_x:
                    dve.tensor_copy(ystage[:, :], Y[:, slot(tl.tile(x)), :]).then_inc(sem("input_staged"), 1)
                if has_v:
                    dve.wait_ge(sem("unit_staged"), part(v, "unit_staged"))
                    dve.bn_stats(st6[:, :], zstage[:, :]).then_inc(sem("unit_stats"), 1)
                    dve.wait_ge(sem("unit_stats"), part(v, "unit_stats"))
                    dve.memset(spare[:, :], 0.0)
                    dve.bn_aggr(mv[:, :], st6[:, :]).then_inc(sem("unit_moments"), 1)
                if has_t:
                    for i in range(2):
                        dve.wait_ge(sem("qk_turned"), part(k, "qk_turned", 2 + i))
                        dve.tensor_copy(kT[k % 2][:, 4 * i:4 * i + 4, WIN:KEYS], four(KT_BANK[i])).then_inc(
                            sem("kT_ready"), 1)
                if has_u:
                    length(0)
                    length(1)
                if has_o:
                    keep_out(0)
                    keep_out(1)
                if has_t:
                    maximum(0)
                    maximum(1)
                if has_u:
                    add_sines(0)
                if has_t:
                    maximum(2)
                if has_x:
                    if k > -2:
                        dve.wait_ge(sem("xT_ready"), part(x - 1, "xT_ready"))
                    dve.wait_ge(sem("x_turned"), part(x, "x_turned"))
                    dve.tensor_copy(xT[x % 2][0:HALF, 0:P], bank[X_BANK][0:HALF, 0:P])
                    dve.tensor_copy(xT[x % 2][HALF:D, 1:P + 1], bank[X_BANK][HALF:D, 0:P])
                    dve.tensor_scalar(xT[x % 2][HALF:D, 0:1], xT[1 - x % 2][HALF:D, P:P + 1],
                                      keepk[HALF:D, bass.ds(tl.tile(x), 1)], None, ALU.mult).then_inc(
                        sem("xT_ready"), 1)
                if k == -2:
                    scale_ropes()
                if has_t:
                    invert(k, 0)
                if has_u:
                    add_sines(1)
                if has_t:
                    maximum(3)
                if has_o:
                    dve.wait_ge(sem("attn_out"), part(o, "attn_out"))
                    so = slot(tl.tile(o))
                    dve.tensor_tensor(Z[:, so, :], bank[WO_BANK][:, 0:D], Y[:, so, :], ALU.add).then_inc(
                        sem("attn_added"), 1)
                if has_t:
                    maximum(4)
                    maximum(5)

            run_steps(dve, tl, step)

        def attention_pool(pool, c, layer):
            tl = Tiles(c * DEPTH * TILES + layer * TILES)
            part = tl.part
            pool.wait_ge(sem("ropes_scaled"), 8 * (c * DEPTH + 1) + 8 * layer)

            def step(k):
                has_x, has_u, has_t, has_o, has_v, has_z = works_on(k)
                u, v = k + 1, k - 2

                def cosine(w):
                    ti = tl.tile(u) & 7
                    if has_t:
                        pool.wait_ge(sem("qk_rotated"), part(k, "qk_rotated", w))
                    pool.wait_ge(sem("proj_copied"), part(u, "proj_copied", 2 * w + 1))
                    pool.tensor_tensor(rot[:, w, :, :], raw[:, w, :, :],
                                       ropes[:, 2 * w, bass.ds(ti, 1), :].broadcast_to([P, HEADS, DH]),
                                       ALU.mult).then_inc(sem("cosine_part"), 1)

                def rnorm(w):
                    pool.wait_ge(sem("norms_squared"), part(u, "norms_squared", w))
                    pool.tensor_tensor(rn[:, 16 * w:16 * w + 16], ss[:, 16 * w:16 * w + 16],
                                       half[:, 16 * w:16 * w + 16], ALU.pow).then_inc(sem("rnorm"), 1)

                if has_u:
                    cosine(0)
                    cosine(1)
                if has_v:
                    pool.wait_ge(sem("unit_moments"), part(v, "unit_moments"))
                    pool.tensor_tensor(rstd1[:, 0:1], mv[:, 1:2], eps[:, 0:1], ALU.add).then_inc(
                        sem("unit_var"), 1)
                    pool.wait_ge(sem("unit_var"), part(v, "unit_var"))
                    pool.tensor_tensor(rstd1[:, 1:2], rstd1[:, 0:1], half[:, 0:1], ALU.pow).then_inc(
                        sem("unit_rstd"), 1)
                if has_u:
                    rnorm(0)
                    rnorm(1)
                if has_t:
                    for j, (h0, h1) in enumerate(NG):
                        pool.wait_ge(sem("inverted"), part(k, "inverted", j))
                        pool.tensor_tensor(prob[:, h0:h1, PADK:2 * P], prob[:, h0:h1, PADK:2 * P],
                                           bc(rden[:, h0:h1], KEYS), ALU.mult).then_inc(
                            sem("normalised"), 1)

            run_steps(pool, tl, step)

        def unit_counts(c, layer, j):
            return c * DEPTH * 4 + layer * 4 + j + 1

        def unit_pe(pe, c, layer):
            pe.wait_ge(sem("unit_weights"), 16 * UW * (c * DEPTH + 1) + 16 * UW * layer)

            def group(j, first):
                n = unit_counts(c, layer, j)
                x = xnT[:, bass.ts(j, 512)]
                for i, (c0, m) in enumerate(FC):
                    for h in (1, 0):
                        pe.matmul(bank[3 * h + i][0:m, :], w1[:, h * DI + c0:h * DI + c0 + m], x,
                                  start=True, stop=True).then_inc(sem("unit_h"), 1)
                if not first:
                    pe.wait_ge(sem("unit_added"), n - 1)
                for i in range(3):
                    m = P if i < 2 else LAST + 1
                    pe.wait_ge(sem("gated"), 3 * (n - 1) + i + 1)
                    for q in range(4):
                        mm = pe.matmul(bank[6][:, P * q:P * q + P], gT[0:m, i, P * q:P * q + P], w2[0:m, i, :],
                                       start=(i == 0 and q == 0), stop=(i == 2), skip_group_check=True)
                mm.then_inc(sem("unit_out"), 1)

            group(0, True)
            with pe.Fori(1, 4) as j:
                group(j, False)

        def unit_act(act, c, layer):
            with act.Fori(0, 4) as j:
                n = unit_counts(c, layer, j)
                for i, (_, m) in enumerate(FC):
                    act.wait_ge(sem("unit_h"), 6 * (n - 1) + 2 * i + 1)
                    act.activation(gel[0:m, i, :], bank[3 + i][0:m, :], ACT.Gelu,
                                   bias=b1[0:m, 3 + i:4 + i]).then_inc(sem("gelu"), 1)

        def unit_dve(dve, c, layer):
            with dve.Fori(0, 4) as j:
                n = unit_counts(c, layer, j)
                for i, (_, m) in enumerate(FC):
                    dve.wait_ge(sem("unit_h"), 6 * (n - 1) + 2 * i + 2)
                    dve.wait_ge(sem("gelu"), 3 * (n - 1) + i + 1)
                    dve.scalar_tensor_tensor(gT[0:m, i, :], bank[i][0:m, :], b1[0:m, i:i + 1],
                                             gel[0:m, i, :], ALU.add, ALU.mult).then_inc(
                        sem("gated"), 1)
                dve.wait_ge(sem("unit_out"), n)
                s = 4 * j + 1 + (j >> 1)
                dve.tensor_tensor(Y[:, bass.ds(s, 4), :], bank[6][:, :].rearrange("p (a b) -> p a b", a=4),
                                  Z[:, bass.ds(s, 4), :], ALU.add).then_inc(sem("unit_added"), 1)

        def stats_dve(dve, n):
            with dve.Fori(0, TILES) as t:
                dve.bn_stats(stt[:, bass.ds(t, 1), :].rearrange("p a b -> p (a b)"),
                             X[:, bass.ds(slot(t), 1), :].rearrange("p a b -> p (a b)")).then_inc(
                    sem("x_stats"), 1)
            dve.wait_ge(sem("x_stats"), TILES * n)
            for t in range(TILES):
                dve.bn_aggr(mva[:, t, :], stt[:, t, :]).then_inc(sem("x_moments"), 1)

        def stats_pool(pool, n):
            pool.wait_ge(sem("x_moments"), TILES * n)
            pool.tensor_tensor(rstda[:, :], mva[:, 0:TILES, 1], eps[:, :], ALU.add).then_inc(sem("x_var"), 1)
            pool.wait_ge(sem("x_var"), n)
            pool.tensor_tensor(rstda[:, :], rstda[:, :], half[:, 0:TILES], ALU.pow).then_inc(sem("x_rstd"), 1)

        def norm_dve(dve, n):
            dve.wait_ge(sem("x_rstd"), n)
            with dve.Fori(0, TILES) as t:
                dve.tensor_scalar(Y[:, bass.ds(slot(t), 1), :].rearrange("p a b -> p (a b)"),
                                  X[:, bass.ds(slot(t), 1), :].rearrange("p a b -> p (a b)"),
                                  mva[:, bass.ds(t, 1), 0:1].rearrange("p a b -> p (a b)"),
                                  rstda[:, bass.ds(t, 1)], ALU.subtract, ALU.mult)

        def norm_tiles_dve(dve, out8, batch, done):
            for i in range(TPB):
                t = TPB * batch + i
                dve.tensor_scalar(out8[:, i, :], X[:, bass.ds((TPB + 1) * batch + 1 + i, 1), :].rearrange(
                    "p a f -> p (a f)"),
                    mva[:, bass.ds(t, 1), 0:1].rearrange("p a b -> p (a b)"), rstda[:, bass.ds(t, 1)],
                    ALU.subtract, ALU.mult).then_inc(sem(done), 1)

        stage8 = aT
        yT8 = qT

        def turn8_pe(pe, name, n8, n):
            for h in range(2):
                pe.wait_ge(sem(name + "_normed"), n8)
                for i in range(4):
                    mm = pe.transpose(bank[h][:, P * i:P * i + P], stage8[:, 4 * h + i, :], ident[:, :])
                mm.then_inc(sem(name + "_turned%d" % h), 1)

        def turn8_act(act, name, n):
            for h in range(2):
                act.wait_ge(sem(name + "_turned%d" % h), n)
                act.activation(yT8[:, 4 * h:4 * h + 4, :], bank[h][:, :].rearrange("p (a b) -> p a b", a=4),
                               ACT.Copy).then_inc(sem(name + "_yT%d" % h), 1)

        def flat8(buf):
            return buf[:, :, :].rearrange("p a b -> p (a b)")

        lin_q = flat8(raw[:, 0, :, :])
        lin_k = raw[:, 1, :, :].rearrange("p h d -> p (h d)").rearrange("p (t f) -> p t f", f=D)
        lin_v = sq[:, 0, :, :].rearrange("p h d -> p (h d)").rearrange("p (t f) -> p t f", f=D)

        def linear_pe(pe):
            with pe.Fori(0, BATCH) as b:
                n = b + 1
                turn8_pe(pe, "lin", TPB * n, n)
                pe.wait_ge(sem("lin_yT0"), n)
                pe.wait_ge(sem("lin_yT1"), n)
                for h in range(2):
                    pe.matmul(bank[2 + h][:, :], wT[:, 0, :], flat8(yT8)[:, 512 * h:512 * h + 512], start=True,
                              stop=True).then_inc(sem("lin_q%d" % h), 1)
                for i in range(TPB):
                    mm = pe.matmul(bank[4 + i // 2][:, 256 * (i % 2):256 * (i % 2) + 256], yT8[:, i, :],
                                   wT[:, 1:3, :].rearrange("p a b -> p (a b)"), start=True, stop=True)
                    if i % 2:
                        mm.then_inc(sem("lin_kv"), 1)
                pe.wait_ge(sem("lin_kv_kept"), n)
                for i in range(TPB):
                    mm = pe.matmul(bank[0][:, 0:D], lin_v[:, i, :], lin_k[:, i, :], start=(i == 0),
                                   stop=(i == TPB - 1))
                mm.then_inc(sem("lin_state"), 1)
                for i in range(TPB):
                    mm = pe.matmul(bank[1][:, 0:1], lin_k[:, i, :], ones[:, :], start=(i == 0),
                                   stop=(i == TPB - 1))
                mm.then_inc(sem("lin_ksum"), 1)
                pe.wait_ge(sem("lin_state_kept"), n)
                pe.matmul(bank[2][:, 0:D], kvT[:, :], wT[:, 3, :], start=True, stop=True).then_inc(
                    sem("lin_mixed"), 1)
                pe.wait_ge(sem("lin_mix_kept"), n)
                for i in range(TPB):
                    mm = pe.matmul(bank[4 + i // 2][:, 256 * (i % 2):256 * (i % 2) + D + 1],
                                   lin_q[:, P * i:P * i + P], mixk[:, :], start=True, stop=True)
                    if i % 2:
                        mm.then_inc(sem("lin_out"), 1)

        def linear_act(act):
            with act.Fori(0, BATCH) as b:
                turn8_act(act, "lin", b + 1)

        def linear_dve(dve):
            with dve.Fori(0, BATCH) as b:
                n = b + 1
                norm_tiles_dve(dve, stage8, b, "lin_normed")
                for h in range(2):
                    dve.wait_ge(sem("lin_q%d" % h), n)
                    dve.tensor_scalar(lin_q[:, 512 * h:512 * h + 512], bank[2 + h][:, :], 0.0, LIN_EPS,
                                      ALU.max, ALU.add).then_inc(sem("lin_q_kept"), 1)
                for i in range(4):
                    dve.wait_ge(sem("lin_kv"), 4 * (n - 1) + i + 1)
                    src = bank[4 + i][:, :].rearrange("p (t a f) -> p t a f", t=2, a=2)
                    dve.tensor_scalar(lin_k[:, 2 * i:2 * i + 2, :], src[:, :, 0, :], 0.0, LIN_EPS, ALU.max, ALU.add)
                    e = dve.tensor_copy(lin_v[:, 2 * i:2 * i + 2, :], src[:, :, 1, :])
                e.then_inc(sem("lin_kv_kept"), 1)
                dve.wait_ge(sem("lin_state"), n)
                dve.tensor_copy(kvT[:, :], bank[0][:, 0:D]).then_inc(sem("lin_state_kept"), 1)
                dve.wait_ge(sem("lin_ksum"), n)
                dve.tensor_copy(mixk[:, D:D + 1], bank[1][:, 0:1])
                dve.wait_ge(sem("lin_mixed"), n)
                dve.tensor_copy(mixk[:, 0:D], bank[2][:, 0:D]).then_inc(sem("lin_mix_kept"), 1)
                for i in range(4):
                    dve.wait_ge(sem("lin_out"), 4 * (n - 1) + i + 1)
                    src = bank[4 + i][:, :].rearrange("p (t f) -> p t f", t=2)
                    dve.tensor_scalar(zden[:, i, :], src[:, :, D], LIN_EPS, None, ALU.add).then_inc(
                        sem("lin_den"), 1)
                    dve.wait_ge(sem("lin_den"), 4 * b + i + 1)
                    dve.reciprocal(zden[:, i, :], zden[:, i, :]).then_inc(sem("lin_inv"), 1)
                    dve.wait_ge(sem("lin_inv"), 4 * b + i + 1)
                    for j in range(2):
                        xs = X[:, bass.ds((TPB + 1) * b + 1 + 2 * i + j, 1), :].rearrange("p a f -> p (a f)")
                        e = dve.scalar_tensor_tensor(xs, src[:, j, 0:D], zden[:, i, j:j + 1], xs, ALU.mult,
                                                     ALU.add).then_inc(sem("lin_added"), 1)
                dve.wait_ge(sem("lin_added"), TPB * n)
                xs = X[:, bass.ds((TPB + 1) * b + 1, TPB), :]
                dve.tensor_tensor(xs, xs, bias[:, 0, :].unsqueeze(1).broadcast_to([P, TPB, D]), ALU.add)

        ex_y = stage8[:, 0:4, :]
        ex_yT = yT8[:, 0:4, :]
        ex_h = raw[:, :, :, :].rearrange("p a h d -> p (a h d)").rearrange("p (m t) -> p m t", m=4)
        ex_g = sq[:, :, :, :].rearrange("p a h d -> p (a h d)").rearrange("p (m t) -> p m t", m=4)
        ex_g2 = rot[:, :, :, :].rearrange("p a h d -> p (a h d)").rearrange("p (m t) -> p m t", m=4)

        def experts_pe(pe, c):
            with pe.Fori(0, 4) as j:
                n = 4 * c + j + 1
                pe.wait_ge(sem("ex_normed"), 4 * n)
                for i in range(4):
                    mm = pe.transpose(bank[0][:, P * i:P * i + P], ex_y[:, i, :], ident[:, :])
                mm.then_inc(sem("ex_turned"), 1)
                pe.wait_ge(sem("ex_yT"), n)
                for i in range(4):
                    mm = pe.matmul(bank[1][:, NE * i:NE * i + NE], ex_yT[:, i, :], wrT[:, :], start=True, stop=True)
                mm.then_inc(sem("ex_logits"), 1)
                for m in range(4):
                    if m >= 2:
                        pe.wait_ge(sem("ex_leaky"), 4 * (n - 1) + (m - 2) + 1)
                    pe.matmul(bank[3 + m % 2][:, :], wT[:, 8 + m, :], ex_yT.rearrange("p a b -> p (a b)"),
                              start=True, stop=True).then_inc(sem("ex_fc"), 1)
                pe.wait_ge(sem("ex_onehot"), n)
                for i in range(4):
                    mm = pe.transpose(bank[2][0:NE, P * i:P * i + P], onehot[:, i, :], ident[:, :])
                mm.then_inc(sem("ex_onehot_turned"), 1)
                pe.wait_ge(sem("ex_onehotT"), n)
                for m in range(4):
                    if m >= 2:
                        pe.wait_ge(sem("ex_gated"), 4 * (n - 1) + (m - 2) + 1)
                    pe.matmul(bank[5 + m % 2][:, :], selb[:, m, :], onehotT[:, :, :].rearrange("p a b -> p (a b)"),
                              start=True, stop=True).then_inc(sem("ex_gate"), 1)
                for m in range(4):
                    pe.wait_ge(sem("ex_squared"), 4 * (n - 1) + m + 1)
                    for i in range(4):
                        mm = pe.matmul(bank[7][:, P * i:P * i + P], ex_g2[:, m, P * i:P * i + P],
                                       wT[:, 12 + m, :], start=(m == 0 and i == 0), stop=(m == 3),
                                       skip_group_check=True)
                mm.then_inc(sem("ex_out"), 1)

        def experts_act(act, c):
            with act.Fori(0, 4) as j:
                n = 4 * c + j + 1
                act.wait_ge(sem("ex_turned"), n)
                act.activation(ex_yT, bank[0][:, :].rearrange("p (a b) -> p a b", a=4), ACT.Copy).then_inc(
                    sem("ex_yT"), 1)
                for m in range(4):
                    act.wait_ge(sem("ex_fc"), 4 * (n - 1) + m + 1)
                    act.activation(ex_h[:, m, :], bank[3 + m % 2][:, :], ACT.Copy, scale=0.5).then_inc(
                        sem("ex_halved"), 1)
                for m in range(4):
                    act.wait_ge(sem("ex_gated"), 4 * (n - 1) + m + 1)
                    act.activation(ex_g2[:, m, :], ex_g[:, m, :], ACT.Square).then_inc(
                        sem("ex_squared"), 1)

        def experts_dve(dve, c):
            with dve.Fori(0, 4) as j:
                n = 4 * c + j + 1
                s = 4 * j + 1 + (j >> 1)
                for i in range(4):
                    dve.tensor_scalar(ex_y[:, i, :], X[:, bass.ds(s + i, 1), :].rearrange("p a f -> p (a f)"),
                                      mva[:, bass.ds(4 * j + i, 1), 0:1].rearrange("p a b -> p (a b)"),
                                      rstda[:, bass.ds(4 * j + i, 1)], ALU.subtract, ALU.mult).then_inc(
                        sem("ex_normed"), 1)
                logits = bank[1][:, 0:4 * NE].rearrange("p (a e) -> p a e", e=NE)
                dve.wait_ge(sem("ex_logits"), n)
                dve.tensor_reduce(lmax[:, :], logits, AX.X, ALU.max).then_inc(sem("ex_lmax"), 1)
                dve.wait_ge(sem("ex_lmax"), n)
                dve.tensor_tensor(cand[:, :, :], logits, bc(lmax[:, :], NE), ALU.is_ge).then_inc(
                    sem("ex_tied"), 1)
                dve.wait_ge(sem("ex_tied"), n)
                dve.tensor_tensor(cand[:, :, :], cand[:, :, :],
                                  erank[:, :].unsqueeze(1).broadcast_to([P, 4, NE]), ALU.mult).then_inc(
                    sem("ex_ranked"), 1)
                dve.wait_ge(sem("ex_ranked"), n)
                dve.tensor_reduce(lmax[:, :], cand[:, :, :], AX.X, ALU.max).then_inc(sem("ex_first"), 1)
                dve.wait_ge(sem("ex_first"), n)
                dve.tensor_tensor(onehot[:, :, :], cand[:, :, :], bc(lmax[:, :], NE), ALU.is_equal).then_inc(
                    sem("ex_onehot"), 1)
                for m in range(4):
                    dve.wait_ge(sem("ex_halved"), 4 * (n - 1) + m + 1)
                    dve.tensor_tensor(ex_h[:, m, :], bank[3 + m % 2][:, :], ex_h[:, m, :], ALU.max).then_inc(
                        sem("ex_leaky"), 1)
                dve.wait_ge(sem("ex_onehot_turned"), n)
                dve.tensor_copy(onehotT[:, :, :], bank[2][0:NE, :].rearrange("p (a b) -> p a b", a=4)).then_inc(
                    sem("ex_onehotT"), 1)
                for m in range(4):
                    dve.wait_ge(sem("ex_leaky"), 4 * (n - 1) + m + 1)
                    dve.wait_ge(sem("ex_gate"), 4 * (n - 1) + m + 1)
                    dve.tensor_tensor(ex_g[:, m, :], bank[5 + m % 2][:, :], ex_h[:, m, :], ALU.mult).then_inc(
                        sem("ex_gated"), 1)
                dve.wait_ge(sem("ex_out"), n)
                xs = X[:, bass.ds(s, 4), :]
                dve.scalar_tensor_tensor(xs, bank[7][:, :].rearrange("p (a b) -> p a b", a=4), 0.5, xs,
                                         ALU.mult, ALU.add)

        at_v = kT[0][:, :, 0:P]
        at_q = raw[:, 0, :, :].rearrange("p h d -> p (h d)")
        at_k = raw[:, 1, :, :].rearrange("p h d -> p (h d)")
        at_p = prob[:, :, :].rearrange("p a b -> p (a b)").rearrange("p (r k) -> p r k", r=GQ)
        at_pT = [b[:, :, :, :].rearrange("p a h d -> p (a h d)").rearrange("p (k r q) -> p k r q", k=4, r=GQ)
                 for b in (rot, qkr)]
        at_o = kT[1][:, :, 0:P]
        at_oT = pTo[:, 0:8, :]
        UNITS = 4 * TPB

        def attention2_pe(pe):
            with pe.Fori(0, BATCH) as b:
                turn8_pe(pe, "at", TPB * (b + 1), b + 1)
                pe.wait_ge(sem("at_yT0"), b + 1)
                pe.wait_ge(sem("at_yT1"), b + 1)
                for h in range(2):
                    for i in range(4):
                        mm = pe.matmul(bank[2 + h][:, P * i:P * i + P], yT8[:, 4 * h + i, :], wT[:, 6, :],
                                       start=True, stop=True)
                    mm.then_inc(sem("at_v%d" % h), 1)
                with pe.Fori(0, 4) as g:
                    ng = 4 * b + g + 1
                    for w in range(2):
                        pe.wait_ge(sem("at_weights%d" % w), ng)
                        for h in range(2):
                            pe.matmul(bank[4 + 2 * w + h][:, :], wst[:, w, :], flat8(yT8)[:, 512 * h:512 * h + 512],
                                      start=True, stop=True).then_inc(sem("at_proj"), 1)
                    pe.wait_ge(sem("at_stacked1"), ng)
                    pe.wait_ge(sem("at_values"), ng)

                    def step(first, at, k):
                        n = first + at + k + 1
                        has_t, has_o = k < TPB, k > 0
                        if has_t:
                            pe.wait_ge(sem("at_qtile"), n)
                            scores2(pe, n, k, 0)
                        if has_o:
                            turn_p2(pe, n - 1, 2)
                        if has_t:
                            scores2(pe, n, k, 1)
                        if has_o:
                            turn_p2(pe, n - 1, 3)
                        if has_t:
                            scores2(pe, n, k, 2)
                        if has_o:
                            pe.wait_ge(sem("at_pT_a"), 4 * (n - 1))
                            pe.wait_ge(sem("at_pT_b"), 4 * (n - 1))
                            for kb in range(NKB):
                                for r in range(GQ):
                                    mm = pe.matmul(bank[4][32 * r:32 * r + 32, 0:P], vg[:, kb, r, :],
                                                   at_pT[kb // 4][:, kb % 4, r, :], start=(kb == 0),
                                                   stop=(kb == NKB - 1), skip_group_check=True)
                            mm.then_inc(sem("at_attended"), 1)
                        if has_t:
                            scores2(pe, n, k, 3)
                        if has_o:
                            pe.wait_ge(sem("at_oT"), n - 1)
                            pe.transpose(bank[6][:, 0:P], oT[:, :], ident[:, :]).then_inc(sem("at_o_turned"), 1)
                        if has_t:
                            turn_p2(pe, n, 0)
                            if has_o:
                                pe.wait_ge(sem("at_o"), n - 1)
                            turn_p2(pe, n, 1)

                    run_units(pe, UNITS * b + TPB * g, step)
                pe.wait_ge(sem("at_o"), UNITS * (b + 1))
                for h in range(2):
                    for i in range(4):
                        mm = pe.transpose(bank[h][:, P * i:P * i + P], at_o[:, 4 * h + i, :], ident[:, :])
                    mm.then_inc(sem("at_all_turned%d" % h), 1)
                for h in range(2):
                    pe.wait_ge(sem("at_all_oT%d" % h), b + 1)
                    for i in range(4):
                        mm = pe.matmul(bank[2 + h][:, P * i:P * i + P], at_oT[:, 4 * h + i, :], wT[:, 7, :],
                                       start=True, stop=True)
                    mm.then_inc(sem("at_out%d" % h), 1)

        def run_units(eng, first, step):
            step(first, 0, 0)
            with eng.Fori(0, TPB - 3, 2) as r:
                step(first, r, 1)
                step(first, r, 2)
            step(first, 0, TPB - 1)
            step(first, 0, TPB)

        def scores2(pe, n, k, r):
            for h in range(2):
                if r >= 2 or k:
                    pe.wait_ge(sem("at_exp"), 4 * (n - 1) + r - 1)
                mm = pe.matmul(bank[2 * (r % 2) + h][:, :], qtile[k % 2][32 * r:32 * r + 32, :],
                               kst[32 * r:32 * r + 32, 512 * h:512 * h + 512], start=True, stop=True)
            mm.then_inc(sem("at_scores"), 1)

        def turn_p2(pe, n, r):
            for h in range(2):
                if r >= 2:
                    pe.wait_ge(sem("at_pT_" + "ab"[h]), 4 * (n - 1) + r - 1)
                pe.wait_ge(sem("at_exp"), 4 * (n - 1) + r + 1)
                for i in range(4):
                    mm = pe.transpose(bank[4 + 2 * (r % 2) + h][:, P * i:P * i + P], at_p[:, r, 512 * h + P * i:512 * h + P * i + P],
                                      ident[:, :])
                mm.then_inc(sem("at_p_turned" + "ab"[h]), 1)

        def attention2_act(act):
            with act.Fori(0, BATCH) as b:
                turn8_act(act, "at", b + 1)
                with act.Fori(0, 4) as g:
                    ng = 4 * b + g + 1
                    for w in range(2):
                        for h in range(2):
                            act.wait_ge(sem("at_proj"), 4 * (ng - 1) + 2 * w + h + 1)
                            act.activation((at_q, at_k)[w][:, 512 * h:512 * h + 512], bank[4 + 2 * w + h][:, :],
                                           ACT.Copy, scale=(float(DK) ** -0.5, 1.0)[w]).then_inc(
                                sem("at_proj_copied%d" % w), 1)

                    def step(first, at, k):
                        n = first + at + k + 1
                        has_t, has_o = k < TPB, k > 0
                        for r in range(GQ if has_t else 1):
                            if has_t:
                                act.wait_ge(sem("at_maxima"), 4 * (n - 1) + r + 1)
                                act.activation(at_p[:, r, :], psum[:, 2 * (r % 2):2 * (r % 2) + 2, :].rearrange(
                                    "p a b -> p (a b)"), ACT.Exp, bias=amax[:, r:r + 1]).then_inc(
                                    sem("at_exp"), 1)
                            if has_o and r == 2:
                                keep_out2(act, n - 1)
                            if has_o and r == 0:
                                keep_pT_act(act, n - 1, 2)
                                keep_pT_act(act, n - 1, 3)
                        if has_t:
                            keep_pT_act(act, n, 0)
                            keep_pT_act(act, n, 1)
                        else:
                            keep_out2(act, n - 1)

                    run_units(act, UNITS * b + TPB * g, step)
                for h in range(2):
                    act.wait_ge(sem("at_all_turned%d" % h), b + 1)
                    act.activation(at_oT[:, 4 * h:4 * h + 4, :], bank[h][:, :].rearrange("p (a b) -> p a b", a=4),
                                   ACT.Copy).then_inc(sem("at_all_oT%d" % h), 1)

        def keep_out2(act, n):
            act.wait_ge(sem("at_attended"), n)
            act.activation(oT[:, :], bank[4][:, 0:P], ACT.Copy).then_inc(sem("at_oT"), 1)

        def keep_pT_act(act, n, r):
            act.wait_ge(sem("at_p_turneda"), 4 * (n - 1) + r + 1)
            act.activation(at_pT[0][:, :, r, :], bank[4 + 2 * (r % 2)][:, :].rearrange("p (a b) -> p a b", a=4),
                           ACT.Copy).then_inc(sem("at_pT_a"), 1)

        def attention2_dve(dve):
            dve.memset(V[1][:, :], 0.0).then_inc(sem("at_zeroed"), 1)
            dve.wait_ge(sem("at_zeroed"), 1)
            dve.memset(vg[:, :, :, DK:DK + 1], 1.0)
            with dve.Fori(0, BATCH) as b:
                norm_tiles_dve(dve, stage8, b, "at_normed")
                for h in range(2):
                    dve.wait_ge(sem("at_v%d" % h), b + 1)
                    dve.tensor_copy(at_v[:, 4 * h:4 * h + 4, :],
                                    bank[2 + h][:, :].rearrange("p (a b) -> p a b", a=4)).then_inc(
                        sem("at_v_kept"), 1)
                with dve.Fori(0, 4) as g:
                    ng = 4 * b + g + 1
                    for w in range(2):
                        src = wT[:, 4 + w, bass.ds(32 * g, 32)].rearrange("p (r d) -> p r d", d=DK)
                        for cpy in range(4):
                            e = dve.tensor_copy(
                                wst[:, w, :].rearrange("p (r c d) -> p r c d", r=GQ, c=4)[:, :, cpy, :], src)
                        e.then_inc(sem("at_weights%d" % w), 1)
                    dve.wait_ge(sem("at_v_kept"), 2 * (b + 1))
                    for r in range(GQ):
                        e = dve.tensor_scalar(vg[:, :, r, 0:DK], at_v[:, :, bass.ds(32 * g + DK * r, DK)], 1.0, None,
                                              ALU.mult)
                    e.then_inc(sem("at_values"), 1)
                    for w in range(2):
                        src, dst = (at_q, at_k)[w], (qst, kst)[w]
                        dve.wait_ge(sem("at_proj_copied%d" % w), 2 * ng)
                        dve.tensor_copy(hi[:, :], src).then_inc(sem("at_high%d" % w), 1)
                        dve.wait_ge(sem("at_high%d" % w), ng)
                        dve.tensor_scalar(sq[:, 1, :, :].rearrange("p h d -> p (h d)"), hi[:, :].bitcast(F32),
                                          stackc[:, 2 * w + 1:2 * w + 2], None, ALU.mult).then_inc(
                            sem("at_high_part%d" % w), 1)
                        dve.wait_ge(sem("at_high_part%d" % w), ng)
                        dve.scalar_tensor_tensor(dst[:, :], src, stackc[:, 2 * w:2 * w + 1],
                                                 sq[:, 1, :, :].rearrange("p h d -> p (h d)"), ALU.mult,
                                                 ALU.add).then_inc(sem("at_stacked%d" % w), 1)
                    dve.wait_ge(sem("at_stacked0"), ng)

                    def stage_queries(n, t, k):
                        dve.tensor_scalar(qtile[k % 2][:, :], qst[:, bass.ts(t, P)].bitcast(F32), 1.0, None,
                                          ALU.mult).then_inc(sem("at_qtile"), 1)

                    stage_queries(UNITS * b + TPB * g + 1, 0, 0)

                    def step(first, at, k):
                        n = first + at + k + 1
                        t = at + k
                        has_t, has_o = k < TPB, k > 0
                        def finish_out():
                            dve.wait_ge(sem("at_o_turned"), n - 1)
                            o = bank[6][:, 0:P].rearrange("p (r c) -> p r c", c=32)
                            dve.reciprocal(orec[:, :], o[:, :, DK]).then_inc(sem("at_orec"), 1)
                            dve.wait_ge(sem("at_orec"), n - 1)
                            dve.tensor_tensor(at_o[:, bass.ds(t - 1, 1), bass.ds(32 * g, 32)].rearrange(
                                "p a (r d) -> p (a r) d", d=DK), o[:, :, 0:DK], bc(orec[:, :], DK),
                                ALU.mult).then_inc(sem("at_o"), 1)

                        if k < TPB - 1:
                            stage_queries(n + 1, t + 1, k + 1)
                        for r in range(GQ if has_t else 1):
                            if has_t:
                                dve.wait_ge(sem("at_scores"), 4 * (n - 1) + r + 1)
                                dve.tensor_reduce(amax[:, r:r + 1],
                                                  psum[:, 2 * (r % 2):2 * (r % 2) + 2, :].rearrange(
                                                      "p a b -> p (a b)"), AX.X, ALU.max, negate=True).then_inc(
                                    sem("at_maxima"), 1)
                            if has_o and r == 0:
                                keep_pT_dve(dve, n - 1, 2)
                                keep_pT_dve(dve, n - 1, 3)
                        if has_o:
                            finish_out()
                        if has_t:
                            keep_pT_dve(dve, n, 0)
                            keep_pT_dve(dve, n, 1)

                    run_units(dve, UNITS * b + TPB * g, step)
                res = lin_k
                for h in range(2):
                    dve.wait_ge(sem("at_out%d" % h), b + 1)
                    dve.tensor_tensor(res[:, 4 * h:4 * h + 4, :], bank[2 + h][:, :].rearrange("p (a b) -> p a b", a=4),
                                      stage8[:, 4 * h:4 * h + 4, :], ALU.add).then_inc(sem("at_res"), 1)
                dve.wait_ge(sem("at_res"), 2 * (b + 1))
                dve.tensor_tensor(res, res, bias[:, 1, :].unsqueeze(1).broadcast_to([P, TPB, D]),
                                  ALU.add).then_inc(sem("at_biased"), 1)
                dve.wait_ge(sem("at_biased"), b + 1)
                for i in range(TPB):
                    e = dve.bn_stats(stt[:, i, :], res[:, i, :])
                e.then_inc(sem("at_stats"), 1)
                dve.wait_ge(sem("at_stats"), b + 1)
                dve.memset(spare[:, :], 0.0)
                for i in range(TPB):
                    e = dve.bn_aggr(mv8[:, i, :], stt[:, i, :])
                e.then_inc(sem("at_moments"), 1)
                dve.wait_ge(sem("at_rstd"), b + 1)
                for i in range(TPB):
                    dve.tensor_scalar(res[:, i, :], res[:, i, :], mv8[:, i, 0:1], rstd8[:, i:i + 1],
                                      ALU.subtract, ALU.mult).then_inc(sem("at_renormed"), 1)
                dve.wait_ge(sem("at_renormed"), TPB * (b + 1))
                dve.tensor_tensor(res, res, bias[:, 2, :].unsqueeze(1).broadcast_to([P, TPB, D]),
                                  ALU.mult).then_inc(sem("at_scaled"), 1)
                dve.wait_ge(sem("at_scaled"), b + 1)
                dve.tensor_tensor(res, res, bias[:, 3, :].unsqueeze(1).broadcast_to([P, TPB, D]),
                                  ALU.add).then_inc(sem("at_shifted"), 1)
                dve.wait_ge(sem("at_shifted"), b + 1)
                xs = X[:, bass.ds((TPB + 1) * b + 1, TPB), :]
                dve.tensor_tensor(xs, xs, res, ALU.add)

        def keep_pT_dve(dve, n, r):
            dve.wait_ge(sem("at_p_turnedb"), 4 * (n - 1) + r + 1)
            dve.tensor_copy(at_pT[1][:, :, r, :], bank[5 + 2 * (r % 2)][:, :].rearrange("p (a b) -> p a b", a=4)).then_inc(
                sem("at_pT_b"), 1)

        def attention2_pool(pool):
            with pool.Fori(0, BATCH) as b:
                pool.wait_ge(sem("at_moments"), b + 1)
                pool.tensor_tensor(rstd8[:, :], mv8[:, :, 1], eps[:, 0:TPB], ALU.add).then_inc(sem("at_var"), 1)
                pool.wait_ge(sem("at_var"), b + 1)
                pool.tensor_tensor(rstd8[:, :], rstd8[:, :], half[:, 0:TPB], ALU.pow).then_inc(sem("at_rstd"), 1)

        block = ctx.enter_context(nc.Block())

        @block.sync
        def _(sp):
            sync_program(sp)

        @block.tensor
        def _(pe):
            pe.wait_ge(sem("const_loaded"), LOADS)
            for i in range(16):
                mm = pe.transpose(bank[i // 4][:, P * (i % 4):P * (i % 4) + P], pTo[:, i, :], ident[:, :])
                mm.then_inc(sem("weights_turned"), 1)
            pe.transpose(bank[4][:, 0:NE], ystage[0:NE, :], ident[0:NE, 0:NE]).then_inc(sem("weights_turned"), 1)
            finish_phase(pe, 1)
            for i, (kind, c) in enumerate(STAGES):
                p0 = first_phase[i]
                finish_phase(pe, p0)
                if kind == "macaron":
                    with pe.Fori(0, DEPTH) as layer:
                        attention_pe(pe, c, layer)
                        finish_phase(pe, p0 + 1 + 2 * layer)
                        unit_pe(pe, c, layer)
                        finish_phase(pe, p0 + 2 + 2 * layer)
                    finish_phase(pe, p0 + 1 + 2 * DEPTH)
                    continue
                if kind == "linear":
                    linear_pe(pe)
                elif kind == "experts":
                    experts_pe(pe, c)
                else:
                    attention2_pe(pe)
                finish_phase(pe, p0 + 1)

        @block.scalar
        def _(act):
            for i in range(4):
                act.wait_ge(sem("weights_turned"), 4 * i + 4)
                act.activation(wT[:, 4 * i:4 * i + 4, :], bank[i][:, :].rearrange("p (a b) -> p a b", a=4), ACT.Copy)
            act.wait_ge(sem("weights_turned"), 17)
            act.activation(wrT[:, :], bank[4][:, 0:NE], ACT.Copy)
            finish_phase(act, 1)
            for i, (kind, c) in enumerate(STAGES):
                p0 = first_phase[i]
                finish_phase(act, p0)
                if kind == "macaron":
                    with act.Fori(0, DEPTH) as layer:
                        attention_act(act, c, layer)
                        finish_phase(act, p0 + 1 + 2 * layer)
                        unit_act(act, c, layer)
                        finish_phase(act, p0 + 2 + 2 * layer)
                    finish_phase(act, p0 + 1 + 2 * DEPTH)
                    continue
                if kind == "linear":
                    linear_act(act)
                elif kind == "experts":
                    experts_act(act, c)
                else:
                    attention2_act(act)
                finish_phase(act, p0 + 1)

        @block.vector
        def _(dve):
            dve.memset(Y[:, :, :], 0.0)
            dve.memset(Z[:, :, :], 0.0)
            dve.memset(prob[:, :, :], 0.0)
            for i in range(2):
                dve.memset(kT[i][:, :, :], 0.0)
                dve.memset(xT[i][:, :], 0.0)
                dve.memset(V[i][:, :], 0.0)
            dve.memset(gT[:, 2, :], 1.0)
            dve.memset(half[:, :], -0.5)
            dve.memset(eps[:, :], LN_EPS)
            dve.memset(carrier[:, :], 0.0)
            dve.memset(ones[:, :], 1.0)
            dve.wait_ge(sem("const_loaded"), LOADS)
            dve.tensor_copy(identb[:, :], ident[:, :])
            dve.tensor_copy(selb[:, :, :], sel[:, :, :])
            for t in range(TILES):
                m = 0 if t % TPB == 0 else 1
                dve.tensor_copy(mask[:, t, :], masks[:, m * KEYS:(m + 1) * KEYS])
            finish_phase_dve(dve, 1)
            for i, (kind, c) in enumerate(STAGES):
                p0 = first_phase[i]
                stats_dve(dve, i + 1)
                if kind == "macaron":
                    norm_dve(dve, i + 1)
                    finish_phase_dve(dve, p0)
                    with dve.Fori(0, DEPTH) as layer:
                        attention_dve(dve, c, layer)
                        finish_phase_dve(dve, p0 + 1 + 2 * layer)
                        unit_dve(dve, c, layer)
                        finish_phase_dve(dve, p0 + 2 + 2 * layer)
                    for b in range(BATCH):
                        dve.scalar_tensor_tensor(rows(X)[:, b], rows(Y)[:, b], 0.5, rows(X)[:, b], ALU.mult, ALU.add)
                    finish_phase_dve(dve, p0 + 1 + 2 * DEPTH)
                    continue
                finish_phase_dve(dve, p0)
                if kind == "linear":
                    linear_dve(dve)
                elif kind == "experts":
                    experts_dve(dve, c)
                else:
                    attention2_dve(dve)
                finish_phase_dve(dve, p0 + 1)

        @block.gpsimd
        def _(pool):
            finish_phase(pool, 1)
            for i, (kind, c) in enumerate(STAGES):
                p0 = first_phase[i]
                stats_pool(pool, i + 1)
                finish_phase(pool, p0)
                if kind == "macaron":
                    with pool.Fori(0, DEPTH) as layer:
                        attention_pool(pool, c, layer)
                        finish_phase(pool, p0 + 1 + 2 * layer)
                        pool.tensor_tensor(carrier[:, 0:1], carrier[:, 1:2], eps[:, 0:1], ALU.mult)
                        finish_phase(pool, p0 + 2 + 2 * layer)
                    finish_phase(pool, p0 + 1 + 2 * DEPTH)
                    continue
                if kind == "attention":
                    attention2_pool(pool)
                finish_phase(pool, p0 + 1)


_INS = ['L0_attn_x', 'L0_attn_W_qkv', 'L0_attn_W_out', 'L0_attn_b_out', 'L0_ffn_Wqkv', 'L0_ffn_q_scale',
        'L0_ffn_k_scale', 'L0_ffn_Wo', 'L0_ffn_ln_g', 'L0_ffn_ln_b', 'L0_ffn_W1', 'L0_ffn_b1', 'L0_ffn_W2',
        'L0_ffn_b2', 'L1_attn_w_q', 'L1_attn_w_k', 'L1_attn_w_v', 'L1_attn_w_o', 'L1_attn_b_o',
        'L1_attn_ln_g', 'L1_attn_ln_b', 'L1_ffn_w_router', 'L1_ffn_w_fc', 'L1_ffn_w_proj']


def shape_constants():
    import numpy as np
    f = np.float32
    tri = np.zeros((P, 400 + 4 * TPB * DH), f)
    tri[:, 0:128] = np.eye(P)
    tri[:, 128:256] = np.eye(P, k=1)
    tri[P - 1, 256] = 1.0
    tri[:, 384:400] = (np.arange(TILES) % TPB != 0)[None, :]
    pair = np.arange(0, DH, 2, dtype=f)
    inv_freq = (f(1.0) / (f(10000.0) ** (pair / f(DH)))).astype(f)
    t = np.arange(SEQ, dtype=f)
    freqs = (t[:, None] * inv_freq[None, :]).astype(f)
    base = ((pair + f(0.4 * DH)) / f(1.4 * DH)).astype(f)
    power = (t - f(SEQ // 2)) / f(WIN // 2)
    scale = (base[None, :] ** power[:, None]).astype(f)
    cos, sin = np.cos(freqs).astype(f), np.sin(freqs).astype(f)
    inv = (f(1.0) / scale).astype(f)
    tabs = [np.concatenate([a, b], -1) for a, b in (
        (f(8.0) * cos * scale, f(8.0) * cos * scale), (-f(8.0) * sin * scale, f(8.0) * sin * scale),
        (cos * inv, cos * inv), (-sin * inv, sin * inv))]
    tri[:, 400:] = np.stack([a.reshape(TPB, P, DH).transpose(1, 0, 2) for a in tabs], 1).reshape(P, -1)
    i = np.arange(P)[:, None]
    j = np.arange(KEYS)[None, :] - WIN
    seen = (j <= i) & (j >= i - WIN)
    masks = np.concatenate([np.where(seen & (j >= 0), 0.0, NEG), np.where(seen, 0.0, NEG)], 1)
    extra = np.zeros((P, NE + 4 + 4 * P), f)
    extra[:, 0:NE] = NE - np.arange(NE)[None, :]
    copy = np.arange(P) // DK % 4
    for w, low in enumerate((copy >= 2, copy % 2 == 1)):
        extra[:, NE + 2 * w] = low
        extra[:, NE + 2 * w + 1] = np.where(low, -1.0, 1.0)
    for m in range(4):
        for e in range(2):
            extra[2 * m + e, NE + 4 + P * m + EH * e:NE + 4 + P * m + EH * e + EH] = 1.0
    return tri, np.concatenate([masks, extra], 1).astype(f)


def kernel(**inputs):
    import numpy as _np
    import concourse.bacc as _bacc
    from concourse import mybir as _mybir
    from concourse.bass_utils import run_bass_kernel_spmd as _run

    nc = _bacc.Bacc("TRN2", target_bir_lowering=False, num_devices=1)
    arrays, args = {}, {}
    consts, masks = shape_constants()
    named = {name: _np.ascontiguousarray(inputs[name]) for name in _INS}
    named["shape_consts"] = consts
    named["shape_masks"] = masks
    for name, a in named.items():
        arrays[f"in_{name}_dram"] = a
        args[name] = nc.dram_tensor(f"in_{name}_dram", a.shape, _mybir.dt.from_np(a.dtype), kind="ExternalInput").ap()
    o = nc.dram_tensor("out_0_dram", (BATCH, SEQ, D), _mybir.dt.float32, kind="ExternalOutput").ap()
    W = {k.replace("L0_ffn_", ""): v for k, v in args.items() if k.startswith("L0_ffn_")}
    W.update({k: v for k, v in args.items() if not k.startswith("L0_ffn_")})
    build(nc, args["L0_attn_x"], W, args["shape_consts"], args["shape_masks"], o)
    r = _run(nc, [arrays], core_ids=[0])
    return r.results[0]["out_0_dram"]
```
